# Optimizing a Trainium2 kernel written in Bass

```python
import numpy as np
import jax
import jax.numpy as jnp

def _softmax(x, axis=-1):
    return jax.nn.softmax(x, axis=axis)

def _gelu(x):
    return jax.nn.gelu(x, approximate=True)

def _silu(x):
    return jax.nn.silu(x)

def _sigmoid(x):
    return jax.nn.sigmoid(x)

def _layernorm(x, axis=-1, eps=1e-05):
    m = jnp.mean(x, axis=axis, keepdims=True)
    v = jnp.var(x, axis=axis, keepdims=True)
    return (x - m) / jnp.sqrt(v + eps)

def _scatter_add(tgt, idx, src, axis=0):
    return tgt.at[idx].add(src)

def _segment_sum(src, seg, n):
    return jax.ops.segment_sum(src, seg, n)
kernel_name = 'mk_adaln_ffn_d1_seqx_r4_4bc706'

def setup_inputs(seed: int=0):
    np.random.seed(seed)
    _w = jnp.asarray

    def _rec_inputs():
        import jax
        import jax.numpy as jnp
        _rk = jax.random.key(seed)
        x = -0.0002928 + 1 * jax.random.normal(jax.random.fold_in(_rk, 1), (8, 256, 256), jnp.float32)
        _lenS = 256 - jax.random.randint(jax.random.fold_in(_rk, 7), (8,), 0, max(1, 256 // 4) + 1, jnp.int32)
        _lenS2 = 256 - jax.random.randint(jax.random.fold_in(_rk, 8), (8,), 0, max(1, 256 // 4) + 1, jnp.int32)
        fside_16xSxS_0 = -5.72187e-05 + 0.999849 * jax.random.normal(jax.random.fold_in(_rk, 11), (16, 256, 256), jnp.float32)
        cond_64 = -0.0265395 + 0.99382 * jax.random.normal(jax.random.fold_in(_rk, 13), (8, 64), jnp.float32)
        _validS = jnp.arange(256)[None, :] < _lenS[:, None]
        _validS2 = jnp.arange(256)[None, :] < _lenS2[:, None]
        _causal = jnp.tril(jnp.ones((256, 256), dtype=bool))
        mask_BxS_bk0 = jnp.logical_not(jnp.broadcast_to(_validS[:, :], (8, 256)))
        return (x, fside_16xSxS_0, cond_64, mask_BxS_bk0)
    x, fside_16xSxS_0, cond_64, mask_BxS_bk0 = _rec_inputs()

    def _L0_cond_setup():
        import jax, jax.numpy as jnp
        import numpy as np
        B, N, DIM, H, DH = (2, 512, 256, 16, 64)
        INNER = H * DH
        EPS = 1e-05

        def layernorm(x, g):
            mean = jnp.mean(x, axis=-1, keepdims=True)
            var = jnp.var(x, axis=-1, keepdims=True)
            return (x - mean) * jax.lax.rsqrt(var + EPS) * g
        key = jax.random.key(seed)
        ks = jax.random.split(key, 10)
        x = jax.random.normal(ks[0], (B, N, DIM), dtype=jnp.float32)
        attn_bias = jax.random.normal(ks[1], (H, N, N), dtype=jnp.float32)
        mask = jax.random.randint(ks[2], (B, N), 0, 2).astype(bool)
        g_in = jnp.ones((DIM,), dtype=jnp.float32)
        null_attn_bias = jax.random.normal(ks[3], (H,), dtype=jnp.float32)
        null_kv = jax.random.normal(ks[4], (2, DH), dtype=jnp.float32)
        Wq = jax.random.normal(ks[5], (DIM, INNER), dtype=jnp.float32) * 0.02
        Wkv = jax.random.normal(ks[6], (DIM, 2 * DH), dtype=jnp.float32) * 0.02
        Wo = jax.random.normal(ks[7], (INNER, DIM), dtype=jnp.float32) * 0.02
        g_out = jnp.ones((DIM,), dtype=jnp.float32)
        return {'x': x, 'attn_bias': attn_bias, 'mask': mask, 'g_in': g_in, 'null_attn_bias': null_attn_bias, 'null_kv': null_kv, 'Wq': Wq, 'Wkv': Wkv, 'Wo': Wo, 'g_out': g_out}
    _L0_cond_all = _L0_cond_setup()
    _L0_cond_in = {k: v for k, v in _L0_cond_all.items() if k in ('g_in', 'null_attn_bias', 'Wq', 'Wkv', 'Wo', 'g_out')}
    del _L0_cond_all

    def _L0_ffn_setup():
        import jax, jax.numpy as jnp
        import numpy as np
        B, S, H, F, G = (8, 512, 256, 1024, 128)
        EPS = 1e-05

        def _dequant(q, scales, g):
            K, N = q.shape
            w = (q.astype(jnp.float32) - 128.0).reshape(K // g, g, N) * scales[:, None, :]
            return w.reshape(K, N)
        key = jax.random.key(seed)
        ks = jax.random.split(key, 8)
        x = jax.random.normal(ks[0], (B, S, H), dtype=jnp.float32)
        ln_gamma = jnp.ones((H,), jnp.float32)
        ln_beta = jnp.zeros((H,), jnp.float32)
        fc1_q = jax.random.randint(ks[1], (H, F), 0, 64, dtype=jnp.int32)
        fc2_q = jax.random.randint(ks[2], (F, H), 0, 64, dtype=jnp.int32)
        fc1_scales = jax.random.uniform(ks[3], (H // G, F), jnp.float32) * 0.02 + 0.001
        fc2_scales = jax.random.uniform(ks[4], (F // G, H), jnp.float32) * 0.02 + 0.001
        fc1_bias = jax.random.normal(ks[5], (F,), jnp.float32) * 0.02
        fc2_bias = jax.random.normal(ks[6], (H,), jnp.float32) * 0.02
        return {'x': x, 'ln_gamma': ln_gamma, 'ln_beta': ln_beta, 'fc1_q': fc1_q, 'fc1_scales': fc1_scales, 'fc1_bias': fc1_bias, 'fc2_q': fc2_q, 'fc2_scales': fc2_scales, 'fc2_bias': fc2_bias}
    _L0_ffn_all = _L0_ffn_setup()
    _L0_ffn_in = {k: v for k, v in _L0_ffn_all.items() if k in ('ln_gamma', 'ln_beta', 'fc1_q', 'fc1_scales', 'fc1_bias', 'fc2_q', 'fc2_scales', 'fc2_bias')}
    del _L0_ffn_all
    return {'x': x, 'fside_16xSxS_0': fside_16xSxS_0, 'cond_64': cond_64, 'mask_BxS_bk0': mask_BxS_bk0, 'L0_cond_g_in': _L0_cond_in['g_in'], 'L0_cond_null_attn_bias': _L0_cond_in['null_attn_bias'], 'L0_cond_Wq': _L0_cond_in['Wq'], 'L0_cond_Wkv': _L0_cond_in['Wkv'], 'L0_cond_Wo': _L0_cond_in['Wo'], 'L0_cond_g_out': _L0_cond_in['g_out'], 'L0_ffn_ln_gamma': _L0_ffn_in['ln_gamma'], 'L0_ffn_ln_beta': _L0_ffn_in['ln_beta'], 'L0_ffn_fc1_q': _L0_ffn_in['fc1_q'], 'L0_ffn_fc1_scales': _L0_ffn_in['fc1_scales'], 'L0_ffn_fc1_bias': _L0_ffn_in['fc1_bias'], 'L0_ffn_fc2_q': _L0_ffn_in['fc2_q'], 'L0_ffn_fc2_scales': _L0_ffn_in['fc2_scales'], 'L0_ffn_fc2_bias': _L0_ffn_in['fc2_bias']}

def reference(x, fside_16xSxS_0, cond_64, mask_BxS_bk0, L0_cond_g_in, L0_cond_null_attn_bias, L0_cond_Wq, L0_cond_Wkv, L0_cond_Wo, L0_cond_g_out, L0_ffn_ln_gamma, L0_ffn_ln_beta, L0_ffn_fc1_q, L0_ffn_fc1_scales, L0_ffn_fc1_bias, L0_ffn_fc2_q, L0_ffn_fc2_scales, L0_ffn_fc2_bias):
    import jax
    import jax.numpy as jnp

    def _L0_cond_ref(x, attn_bias, mask, g_in, null_attn_bias, null_kv, Wq, Wkv, Wo, g_out):
        import jax, jax.numpy as jnp
        import numpy as np
        B, N, DIM, H, DH = (2, 512, 256, 16, 64)
        INNER = H * DH
        EPS = 1e-05

        def layernorm(x, g):
            mean = jnp.mean(x, axis=-1, keepdims=True)
            var = jnp.var(x, axis=-1, keepdims=True)
            return (x - mean) * jax.lax.rsqrt(var + EPS) * g
        b, n, _ = x.shape
        scale = DH ** (-0.5)
        xn = layernorm(x, g_in)
        q = (xn @ Wq).reshape(b, n, H, DH).transpose(0, 2, 1, 3) * scale
        kv = xn @ Wkv
        k, v = (kv[..., :DH], kv[..., DH:])
        nk = jnp.broadcast_to(null_kv[0], (b, 1, DH))
        nv = jnp.broadcast_to(null_kv[1], (b, 1, DH))
        k = jnp.concatenate([nk, k], axis=1)
        v = jnp.concatenate([nv, v], axis=1)
        sim = jnp.einsum('bhid,bjd->bhij', q, k)
        null_col = jnp.broadcast_to(null_attn_bias[:, None, None], (H, n, 1))
        bias = jnp.concatenate([null_col, attn_bias], axis=-1)
        sim = sim + bias
        neg = -jnp.finfo(sim.dtype).max
        j = n + 1
        causal_mask = jnp.triu(jnp.ones((n, j), dtype=bool), k=j - n + 1)
        sim = jnp.where(causal_mask, neg, sim)
        mask_p = jnp.pad(mask, ((0, 0), (1, 0)), constant_values=True)
        sim = jnp.where(mask_p[:, None, None, :], sim, neg)
        attn = jax.nn.softmax(sim, axis=-1)
        out = jnp.einsum('bhij,bjd->bhid', attn, v)
        out = out.transpose(0, 2, 1, 3).reshape(b, n, INNER)
        out = out @ Wo
        return layernorm(out, g_out)

    def _L0_ffn_ref(x, ln_gamma, ln_beta, fc1_q, fc1_scales, fc1_bias, fc2_q, fc2_scales, fc2_bias):
        import jax, jax.numpy as jnp
        import numpy as np
        B, S, H, F, G = (8, 512, 256, 1024, 128)
        EPS = 1e-05

        def _dequant(q, scales, g):
            K, N = q.shape
            w = (q.astype(jnp.float32) - 128.0).reshape(K // g, g, N) * scales[:, None, :]
            return w.reshape(K, N)
        residual = x
        mu = jnp.mean(x, axis=-1, keepdims=True)
        var = jnp.mean(jnp.square(x - mu), axis=-1, keepdims=True)
        h = (x - mu) * jax.lax.rsqrt(var + EPS) * ln_gamma + ln_beta
        hf = h.reshape(-1, H)
        w1 = _dequant(fc1_q, fc1_scales, G)
        y = hf @ w1 + fc1_bias
        y = jax.nn.silu(y)
        w2 = _dequant(fc2_q, fc2_scales, G)
        z = y @ w2 + fc2_bias
        return residual + 0.5 * z.reshape(residual.shape)
    x = x + _L0_ffn_ref(_L0_cond_ref(x, fside_16xSxS_0, mask_BxS_bk0, L0_cond_g_in, L0_cond_null_attn_bias, cond_64, L0_cond_Wq, L0_cond_Wkv, L0_cond_Wo, L0_cond_g_out), L0_ffn_ln_gamma, L0_ffn_ln_beta, L0_ffn_fc1_q, L0_ffn_fc1_scales, L0_ffn_fc1_bias, L0_ffn_fc2_q, L0_ffn_fc2_scales, L0_ffn_fc2_bias)
    return x

_drawn_inputs = setup_inputs


def setup_inputs(seed=0):
    import zlib

    import numpy as np

    out = dict(_drawn_inputs(seed))
    spreads = {'L0_cond_g_in': (1.0, 0.2),
     'L0_cond_g_out': (1.0, 0.2),
     'L0_ffn_ln_gamma': (1.0, 0.2),
     'L0_ffn_ln_beta': (0.0, 0.1)}
    factors = {}
    for name, (base, spread) in spreads.items():
        noise = np.random.default_rng([zlib.crc32(name.encode()), seed]).standard_normal(out[name].shape)
        drawn = base * np.exp(spread * noise) if base else spread * noise
        out[name] = jnp.asarray(drawn.astype(out[name].dtype))
    for name, factor in factors.items():
        out[name] = (out[name] * factor).astype(out[name].dtype)
    return out
```

```python
from contextlib import ExitStack

import concourse.bass as bass
from concourse import mybir

ALU = mybir.AluOpType
ACT = mybir.ActivationFunctionType
F32 = mybir.dt.float32
F32R = mybir.dt.float32r
I32 = mybir.dt.int32
U8 = mybir.dt.uint8

P = 128
B, N, DIM = 8, 256, 256
H, DH = 16, 64
INNER = H * DH
F = 1024
EPS = 1e-5
BIG = 1.0e38
PAIRS = H // 2
KD = DIM // P
TT = N // P
FM = F // P
C0 = 1 + P
C1 = 1 + N
CS = C0 + C1
RING = 8

JOBS = [("F2", 0), ("F2", 1), ("W", 0), ("X", 0), ("W", 1), ("Q", 0), ("Q", 1), ("HT", 0),
        ("F1", 0), ("F1", 1), ("F1", 2), ("F1", 3), ("Q", 2), ("KV", 0), ("Q", 3)]
PER = {"F2": 2, "W": 2, "X": 1, "Q": 4, "HT": 1, "F1": 4, "KV": 1, "BT": 1}
LAG = {"F2": 2, "W": 1, "HT": 1, "F1": 1, "X": -1, "Q": -1, "KV": -1}
FILL_A = {0: [0], 1: [1], 2: [2], 3: [4], 4: [5], 5: [7], 6: [10, 11], 7: [13]}
FILL_B = {2: [3], 4: [6], 5: [8, 9], 6: [12], 7: [14]}
G_BANKS = 3


def runs(kind, b):
    return not isinstance(b, int) or 0 <= b - LAG[kind] < B


def count(kind, j, b):
    return PER[kind] * (b - LAG[kind]) + j + 1


def bank_before(i, b):
    while True:
        i -= G_BANKS
        if i < 0:
            i += len(JOBS)
            b = b - 1
            if isinstance(b, int) and b < -1:
                return None
        kind, j = JOBS[i]
        if isinstance(b, int) and b == 0 and (kind, j) == ("HT", 0):
            return "BT", 1
        if runs(kind, b):
            return kind, count(kind, j, b)


def build(nc, x, bias_rows, mask_rows, wq, wkv, wo, q1, s1, q2, s2, columns, rows, out):
    with ExitStack() as ctx:
        def sb(name, shape, dt=F32):
            return ctx.enter_context(nc.sbuf_tensor(name, shape, dt))

        def psum(name, shape, dt=F32):
            return ctx.enter_context(nc.psum_tensor(name, shape, dt))

        def sem(name):
            return ctx.enter_context(nc.semaphore(name))

        wq_h, wq_l = sb("wq_h", [P, KD, INNER], F32R), sb("wq_l", [P, KD, INNER], F32R)
        wk_h, wk_l = sb("wk_h", [P, KD, P], F32R), sb("wk_l", [P, KD, P], F32R)
        wv_h, wv_l = sb("wv_h", [P, KD, DH], F32R), sb("wv_l", [P, KD, DH], F32R)
        wo_h, wo_l = sb("wo_h", [P, PAIRS, DIM], F32R), sb("wo_l", [P, PAIRS, DIM], F32R)
        w1_h, w1_l = sb("w1_h", [P, KD, F], F32R), sb("w1_l", [P, KD, F], F32R)
        w2_h, w2_l = sb("w2_h", [P, FM, DIM], F32R), sb("w2_l", [P, FM, DIM], F32R)
        xT_h, xT_l = sb("xT_h", [P, KD, N], F32R), sb("xT_l", [P, KD, N], F32R)
        hT_h, hT_l = sb("hT_h", [P, KD, N], F32R), sb("hT_l", [P, KD, N], F32R)
        q_sb, k_sb = sb("q_sb", [P, PAIRS, N]), sb("k_sb", [P, 1 + N])
        o_h, o_l = sb("o_h", [P, PAIRS, N], F32R), sb("o_l", [P, PAIRS, N], F32R)
        y_h, y_l = sb("y_h", [P, FM, N], F32R), sb("y_l", [P, FM, N], F32R)
        bias = sb("bias", [P, H, CS])
        maskrow = sb("maskrow", [P, CS])
        mask_words = sb("mask_words", [P, N // 4], I32)
        score = sb("score", [P, RING, CS])
        neg_max = sb("neg_max", [P, RING, 2])
        denom = sb("denom", [P, RING, 2])
        rdenom = sb("rdenom", [P, RING, 2])
        pT = sb("pT", [P, 4, N + P])
        v_next = sb("v_next", [P, TT, DH])
        v_live = sb("v_live", [P, TT, DH])
        xs = sb("xs", [P, TT, DIM])
        xn = sb("xn", [P, TT, DIM])
        scratch = sb("scratch", [P, 16, DIM])
        u_buf = scratch[:, 0:4, :].rearrange("p (r m) n -> p r m n", r=2)
        t_buf = scratch[:, 4:8, :].rearrange("p (r m) n -> p r m n", r=2)
        hid = scratch[:, 8:10, :]
        hn = scratch[:, 10:12, :]
        base = scratch[:, 12:14, :]
        xres = scratch[:, 14:16, :]
        w_raw = [scratch[:, 4 * i:4 * i + 4, :].rearrange("p a n -> p (a n)") for i in range(2)]
        s_raw = [scratch[:, 8 + 4 * i:12 + 4 * i, :].rearrange("p a n -> p (a n)") for i in range(2)]
        out_sb = sb("out_sb", [P, TT, DIM])
        row_sb = sb("row_sb", [P, 2 * DIM + DH])
        gout_row, b2_row, nv_row = (row_sb[:, 0:DIM], row_sb[:, DIM:2 * DIM],
                                    row_sb[:, 2 * DIM:2 * DIM + DH])
        wkv_raw = sb("wkv_raw", [P, KD, 2 * DH])
        col_sb = sb("col_sb", [P, 3 * KD + FM + 2])
        gin_col, gam_col, bet_col = (col_sb[:, KD * i:KD * (i + 1)] for i in range(3))
        b1_col = col_sb[:, 3 * KD:3 * KD + FM]
        nk_col, nv_col = (col_sb[:, 3 * KD + FM + i:3 * KD + FM + i + 1] for i in range(2))
        ident = sb("ident", [P, P])
        halves = sb("halves", [P, TT])
        x_st, x_mv, x_var, x_rs = (sb("x_st", [P, TT, 6]), sb("x_mv", [P, TT, 2]),
                                   sb("x_var", [P, TT]), sb("x_rs", [P, TT]))
        a_st, a_mv, a_var, a_rs = (sb("a_st", [P, TT, 6]), sb("a_mv", [P, TT, 2]),
                                   sb("a_var", [P, TT]), sb("a_rs", [P, TT]))
        h_st, h_mv, h_var, h_rs = (sb("h_st", [P, TT, 6]), sb("h_mv", [P, TT, 2]),
                                   sb("h_var", [P, TT]), sb("h_rs", [P, TT]))

        S_ps = [psum(f"S_ps{i}", [P, 512]) for i in range(2)]
        T_ps = [psum(f"T_ps{i}", [P, 512]) for i in range(2)]
        O_ps = psum("O_ps", [P, 512])
        G_ps = [psum(f"G_ps{i}", [P, 512]) for i in range(G_BANKS)]

        def view(t):
            return t.bitcast(F32)

        x_in, xres_in, mask_in = sem("x_in"), sem("xres_in"), sem("mask_in")
        cols_in, wkv_in, wq_in = sem("cols_in"), sem("wkv_in"), [sem("wq_in0"), sem("wq_in1")]
        rows_in = sem("rows_in")
        stage_in = [sem("stage_in0"), sem("stage_in1")]
        bias_in = [sem(f"bias_in{i}") for i in range(4)]
        out_sent = sem("out_sent")
        wkv_hi, wkv_done = sem("wkv_hi"), sem("wkv_done")
        chunk_deq, chunk_hi, chunk_done = sem("chunk_deq"), sem("chunk_hi"), sem("chunk_done")
        ident_zero, ident_done, nk_done = sem("ident_zero"), sem("ident_done"), sem("nk_done")
        causal_done, halves_done, mask_edge = sem("causal_done"), sem("halves_done"), sem("mask_edge")
        b2_half, b1_done = sem("b2_half"), sem("b1_done")
        mask_ready, score_bias = sem("mask_ready"), sem("score_bias")
        scores_done, shifted, exp_done = sem("scores_done"), sem("shifted"), sem("exp_done")
        rdenom_done, even_done, odd_done, trans_done = (
            sem("rdenom_done"), sem("even_done"), sem("odd_done"), sem("trans_done"))
        pT_even, pT_odd, pv_done = sem("pT_even"), sem("pT_odd"), sem("pv_done")
        o_hi, o_split, v_ready = sem("o_hi"), sem("o_split"), sem("v_ready")
        full = {k: sem(f"{k}_full") for k in ("F2", "W", "X", "Q", "HT", "F1", "KV", "BT")}
        xT_hi, hT_hi, k_ready = sem("xT_hi"), sem("hT_hi"), sem("k_ready")
        q_ready, kv_ready, xT_split, hT_split = (
            sem("q_ready"), sem("kv_ready"), sem("xT_split"), sem("hT_split"))
        a_normed, u_ready, out_ready = sem("a_normed"), sem("u_ready"), sem("out_ready")
        emptied = {"F2": out_ready, "W": a_normed, "X": xT_split, "Q": q_ready, "HT": hT_split,
                   "F1": u_ready, "KV": kv_ready, "BT": b1_done}
        x_stats, x_aggr, x_vare, x_rstd, xn_ready = (
            sem("x_stats"), sem("x_aggr"), sem("x_vare"), sem("x_rstd"), sem("xn_ready"))
        a_stats, a_aggr, a_vare, a_rstd = sem("a_stats"), sem("a_aggr"), sem("a_vare"), sem("a_rstd")
        h_ready, base_x, base_ready = sem("h_ready"), sem("base_x"), sem("base_ready")
        h_stats, h_aggr, h_vare, h_rstd, hn_ready = (
            sem("h_stats"), sem("h_aggr"), sem("h_vare"), sem("h_rstd"), sem("hn_ready"))
        tanh_done, y_ready, y_hi, y_split = (
            sem("tanh_done"), sem("y_ready"), sem("y_hi"), sem("y_split"))

        dve_passed, pool_passed, pe_passed = sem("dve_passed"), sem("pool_passed"), sem("pe_passed")

        block = ctx.enter_context(nc.Block())

        def batches(eng, batch):
            batch(-1)
            batch(0)
            batch(1)
            with eng.Fori(2, B - 1) as b:
                batch(b)
            batch(B - 1)
            batch(B)
            batch(B + 1)

        def inside(b, lo, hi):
            return not isinstance(b, int) or lo <= b <= hi

        def attends(b):
            return inside(b, 0, B - 1)

        def pair_runs(b, p):
            return not isinstance(b, int) or 0 <= PAIRS * b + p < PAIRS * B

        def gate(eng, passed):
            eng.sem_inc(passed, 1)

        def chunk_src(c):
            if c < 2:
                return wq[c * P:(c + 1) * P, :]
            if c < 4:
                r = wo.rearrange("(a p) n -> p a n", p=P)
                return r[:, 4 * (c - 2):4 * (c - 1), :]
            if c < 6:
                return q1[(c - 4) * P:(c - 3) * P, :]
            r = q2.rearrange("(a p) n -> p a n", p=P)
            return r[:, 4 * (c - 6):4 * (c - 5), :]

        def chunk_scales(c):
            if c < 6:
                return s1[c - 4:c - 3, :].broadcast_to([P, F])
            r = s2[4 * (c - 6):4 * (c - 5), :]
            return r.rearrange("(o g) n -> o g n", o=1).broadcast_to([P, 4, DIM])

        def chunk_dst(c):
            if c < 2:
                return wq_h[:, c, :], wq_l[:, c, :]
            if c < 4:
                s = slice(4 * (c - 2), 4 * (c - 1))
                return (wo_h[:, s, :].rearrange("p a n -> p (a n)"),
                        wo_l[:, s, :].rearrange("p a n -> p (a n)"))
            if c < 6:
                return w1_h[:, c - 4, :], w1_l[:, c - 4, :]
            s = slice(4 * (c - 6), 4 * (c - 5))
            return (w2_h[:, s, :].rearrange("p a n -> p (a n)"),
                    w2_l[:, s, :].rearrange("p a n -> p (a n)"))

        def chunk_scale(c):
            if c < 2:
                return gin_col[:, c:c + 1]
            if c < 4:
                return 1.0
            if c < 6:
                return gam_col[:, c - 4:c - 3]
            return 0.25

        BIAS_HEADS = [(0, 2), (2, 4), (4, 8), (8, 16)]

        @block.sync
        def _(sp):
            def load_x(b):
                rows = x[b] if isinstance(b, int) else x[bass.ds(b, 1)].rearrange("o r c -> (o r) c")
                sp.dma_start(xs[:, :, :], rows.rearrange("(t p) c -> p t c", p=P)).then_inc(x_in, 16)

            def load_mask(b):
                src = mask_rows[b:b + 1, :] if isinstance(b, int) else mask_rows[bass.ds(b, 1), :]
                sp.dma_start(mask_words[:, :], src.broadcast_to([P, N // 4])).then_inc(mask_in, 16)

            def load_chunk(c):
                if c >= 2:
                    sp.wait_ge(chunk_done, c - 1)
                dst = w_raw[c % 2] if c < 4 else w_raw[c % 2].bitcast(I32)
                if 2 <= c < 4 or c >= 6:
                    dst = dst.rearrange("p (a n) -> p a n", a=4)
                if c >= 6:
                    sp.wait_ge(full["BT"], 1)
                sp.dma_start(dst, chunk_src(c)).then_inc(stage_in[c % 2], 16)
                if c >= 4:
                    d = s_raw[c % 2]
                    if c >= 6:
                        d = d.rearrange("p (a n) -> p a n", a=4)
                    sp.dma_start(d, chunk_scales(c)).then_inc(stage_in[c % 2], 16)

            def batch(b):
                if isinstance(b, int) and b == -1:
                    load_x(0)
                    sp.dma_start(wkv_raw[:, :, :], wkv.rearrange("(a p) n -> p a n", p=P)).then_inc(wkv_in, 16)
                    load_chunk(0)
                    load_chunk(1)
                    sp.wait_ge(xn_ready, 1)
                    load_x(1)
                    sp.wait_ge(mask_ready, 1)
                    load_mask(1)
                    for c in range(2, 8):
                        load_chunk(c)
                    return
                if inside(b, 1, B - 2):
                    sp.wait_ge(xn_ready, b + 1)
                    load_x(b + 1)
                if inside(b, 1, B):
                    if not (isinstance(b, int) and b == 1):
                        sp.wait_ge(base_x, TT * (b - 1))
                    else:
                        sp.wait_ge(chunk_done, 8)
                    rows = x[b - 1] if isinstance(b, int) else \
                        x[bass.ds(b - 1, 1)].rearrange("o r c -> (o r) c")
                    sp.dma_start(xres, rows.rearrange("(t p) c -> p t c", p=P)).then_inc(xres_in, 16)
                if inside(b, 1, B - 2):
                    sp.wait_ge(mask_ready, b + 1)
                    load_mask(b + 1)
                if inside(b, 2, B + 1):
                    for t in range(TT):
                        sp.wait_ge(out_ready, TT * (b - 2) + t + 1)
                        rows = out[b - 2] if isinstance(b, int) else \
                            out[bass.ds(b - 2, 1)].rearrange("o r c -> (o r) c")
                        sp.dma_start(rows[t * P:(t + 1) * P, :], out_sb[:, t, :]).then_inc(out_sent, 16)

            batches(sp, batch)
            sp.wait_ge(out_sent, 16 * B * TT)

        @block.gpsimd
        def _(pool):
            g = nc.gpsimd

            def convert_mask(b):
                pool.wait_ge(mask_in, 16 * (b + 1))
                if not isinstance(b, int) or b > 0:
                    pool.wait_ge(score_bias, H * b)
                    gate(pool, pool_passed)
                for a, w in ((1, P), (C0 + 1, N)):
                    i = g.tensor_scalar(maskrow[:, a:a + w], mask_words[:, :].bitcast(U8)[:, 0:w], -BIG, BIG, ALU.mult, ALU.add)
                i.then_inc(mask_ready, 1)

            def bias_scores(b, p):
                for i in range(2):
                    h = 2 * p + i
                    if isinstance(b, int) and b == 0:
                        group = [n for n, (lo, hi) in enumerate(BIAS_HEADS) if lo <= h < hi][0]
                        pool.wait_ge(bias_in[group], 16)
                        fresh = i == 0
                        if fresh:
                            for a in (1, C0 + 1 + P):
                                blk = bias[:, h:h + 2, a:a + P]
                                c = g.affine_select(out=blk, in_=blk, pattern=[[0, 2], [-1, P]],
                                                    compare_op=ALU.is_ge, fill=-BIG, base=0,
                                                    channel_multiplier=1)
                                c.then_inc(causal_done, 1)
                        pool.wait_ge(causal_done, 2 * (p + 1))
                    if not (isinstance(b, int) and b == 0 and h < RING):
                        pool.wait_ge(trans_done, PAIRS * b + p - RING // 2 + 1)
                    if i == 0:
                        pool.wait_ge(mask_ready, b + 1)
                    g.tensor_tensor(score[:, h % RING, :], maskrow[:, :], bias[:, h, :],
                                    ALU.subtract).then_inc(score_bias, 1)

            def power(out_, in_, n):
                return g.tensor_tensor(out_, in_, halves[:, 0:n], ALU.pow)

            def h_rows(b, t):
                pool.wait_ge(a_normed, TT * (b - 1) + t + 1)
                g.tensor_tensor(hid[:, t, :], hid[:, t, :], gout_row[:, :], ALU.mult).then_inc(h_ready, 1)

            def base_rows(b, t):
                if t == 0:
                    pool.wait_ge(xres_in, 16 * b)
                    if not (isinstance(b, int) and b < 2):
                        pool.wait_ge(out_ready, TT * (b - 1))
                    else:
                        pool.wait_ge(b2_half, 1)
                g.tensor_tensor(base[:, t, :], xres[:, t, :], b2_row[:, :], ALU.add).then_inc(base_x, 1)
                pool.wait_ge(base_x, TT * (b - 1) + t + 1)
                pool.wait_ge(h_ready, TT * (b - 1) + t + 1)
                g.tensor_tensor(base[:, t, :], base[:, t, :], hid[:, t, :], ALU.add).then_inc(base_ready, 1)

            def y_low(b, j):
                pool.wait_ge(y_hi, 4 * (b - 1) + j + 1)
                g.tensor_tensor(y_l[:, 2 * j:2 * j + 2, :], t_buf[:, j % 2], view(y_h[:, 2 * j:2 * j + 2, :]),
                                ALU.subtract).then_inc(y_split, 1)

            def x_power(b):
                pool.wait_ge(x_vare, b + 2)
                power(x_rs[:, :], x_var[:, :], TT).then_inc(x_rstd, 1)

            def batch(b):
                if isinstance(b, int) and b == -1:
                    g.memset(halves[:, :], -0.5).then_inc(halves_done, 1)
                    g.memset(maskrow[:, 0:CS:C0], 0.0).then_inc(mask_edge, 1)
                    g.memset(ident[:, :], 0.0).then_inc(ident_zero, 1)
                    pool.wait_ge(ident_zero, 1)
                    g.affine_select(out=ident[:, :], in_=ident[:, :], compare_op=ALU.not_equal, fill=1.0,
                                    base=0, pattern=[[-1, P]], channel_multiplier=1).then_inc(ident_done, 1)
                    pool.wait_ge(halves_done, 1)
                    x_power(b)
                    pool.wait_ge(mask_edge, 1)
                    convert_mask(0)
                    bias_scores(0, 0)
                    return
                for p in range(PAIRS):
                    if attends(b):
                        if p < PAIRS - 1:
                            bias_scores(b, p + 1)
                        elif inside(b, 0, B - 2):
                            convert_mask(b + 1)
                            bias_scores(b + 1, 0)
                    if inside(b, 0, B - 2) and p == 0:
                        x_power(b)
                    if inside(b, 1, B):
                        if p == 2:
                            pool.wait_ge(a_vare, TT * (b - 1) + 1)
                            power(a_rs[:, 0:1], a_var[:, 0:1], 1).then_inc(a_rstd, 1)
                        if p == 3:
                            h_rows(b, 0)
                            pool.wait_ge(a_vare, TT * (b - 1) + 2)
                            power(a_rs[:, 1:2], a_var[:, 1:2], 1).then_inc(a_rstd, 1)
                            base_rows(b, 0)
                        if p == 4:
                            h_rows(b, 1)
                            pool.wait_ge(h_vare, TT * (b - 1) + 1)
                            power(h_rs[:, 0:1], h_var[:, 0:1], 1).then_inc(h_rstd, 1)
                            pool.wait_ge(h_vare, TT * (b - 1) + 2)
                            power(h_rs[:, 1:2], h_var[:, 1:2], 1).then_inc(h_rstd, 1)
                            base_rows(b, 1)
                        if p == 6:
                            y_low(b, 0)
                            y_low(b, 1)
                        if p == 7:
                            y_low(b, 2)
                            y_low(b, 3)

            batches(pool, batch)

        @block.scalar
        def _(act):
            a = nc.scalar

            def high(kind, j, b):
                bank = G_ps[JOBS.index((kind, j)) % G_BANKS]
                act.wait_ge(full[kind], count(kind, j, b))
                if kind == "X":
                    if not (isinstance(b, int) and b == -1):
                        act.wait_ge(full["Q"], 4 * (b + 1))
                    a.activation(xT_h[:, :, :].rearrange("p a n -> p (a n)"), bank[:, :],
                                 ACT.Copy).then_inc(xT_hi, 1)
                elif kind == "HT":
                    if not (isinstance(b, int) and b == 1):
                        act.wait_ge(full["F1"], 4 * (b - 1))
                    a.activation(hT_h[:, :, :].rearrange("p a n -> p (a n)"), bank[:, :],
                                 ACT.Copy).then_inc(hT_hi, 1)
                elif kind == "Q":
                    if not (isinstance(b, int) and b == -1):
                        act.wait_ge(scores_done, PAIRS * b + 2 * j + 2)
                    a.activation(q_sb[:, 2 * j:2 * j + 2, :].rearrange("p a n -> p (a n)"), bank[:, :],
                                 ACT.Copy, scale=-DH ** -0.5).then_inc(q_ready, 1)
                elif kind == "KV":
                    if not (isinstance(b, int) and b == -1):
                        act.wait_ge(scores_done, PAIRS * (b + 1))
                    a.activation(k_sb[:, 1:N + 1], bank[:, 0:N], ACT.Copy).then_inc(k_ready, 1)

            def hidden(j, b):
                n = 4 * (b - 1) + j
                act.wait_ge(u_ready, n + 1)
                if not (isinstance(b, int) and b == 1 and j < 2):
                    act.wait_ge(y_split, n - 1)
                elif j == 0:
                    act.wait_ge(chunk_done, 8)
                a.activation(t_buf[:, j % 2], u_buf[:, j % 2], ACT.Tanh, scale=0.5).then_inc(tanh_done, 1)

            def hidden_high(j, b):
                act.wait_ge(y_ready, 4 * (b - 1) + j + 1)
                if j == 0 and not (isinstance(b, int) and b == 1):
                    act.wait_ge(full["F2"], TT * (b - 1))
                a.activation(y_h[:, 2 * j:2 * j + 2, :], t_buf[:, j % 2], ACT.Copy).then_inc(y_hi, 1)

            def exponentials(b, p):
                for i in range(2):
                    s = (2 * p + i) % RING
                    for qt, (c, w) in enumerate(((0, C0), (C0, C1))):
                        act.wait_ge(shifted, 4 * (PAIRS * b + p) + 2 * i + qt + 1)
                        a.activation(score[:, s, c:c + w], score[:, s, c:c + w], ACT.Exp,
                                     bias=neg_max[:, s, qt:qt + 1], scale=-1.0,
                                     accum_out=denom[:, s, qt:qt + 1]).then_inc(exp_done, 1)

            def normalise_even(b, p):
                s = (2 * p) % RING
                act.wait_ge(rdenom_done, PAIRS * b + p + 1)
                for qt, (c, w) in enumerate(((1, P), (C0 + 1, N))):
                    i = a.activation(score[:, s, c:c + w], score[:, s, c:c + w], ACT.Copy,
                                     scale=rdenom[:, s, qt:qt + 1])
                i.then_inc(even_done, 1)

            def even_transposed(b, p):
                n = PAIRS * b + p
                act.wait_ge(trans_done, n + 1)
                if not (isinstance(b, int) and n < 2):
                    act.wait_ge(pv_done, n - 1)
                a.activation(pT[:, 2 * (p % 2), :], T_ps[0][:, 0:N + P], ACT.Copy).then_inc(pT_even, 1)

            def o_high(b, p):
                n = PAIRS * b + p
                act.wait_ge(pv_done, n + 1)
                if p % PAIRS == 0 and not (isinstance(b, int) and n < PAIRS):
                    act.wait_ge(full["W"], TT * (b if p >= 0 else b - 1))
                a.activation(o_h[:, p % PAIRS, :], O_ps[:, 0:N], ACT.Identity,
                             bias=nv_col[:, :]).then_inc(o_hi, 1)

            def split_chunk(c):
                dst, _ = chunk_dst(c)
                if c < 4:
                    act.wait_ge(stage_in[c % 2], 16 * (c // 2 + 1))
                else:
                    act.wait_ge(chunk_deq, c - 3)
                func = ACT.Copy if isinstance(chunk_scale(c), float) else ACT.Identity
                a.activation(dst, w_raw[c % 2], func, scale=chunk_scale(c)).then_inc(chunk_hi, 1)

            def batch(b):
                if isinstance(b, int) and b == -1:
                    act.dma_start(col_sb[:, :], columns).then_inc(cols_in, 16)
                    act.dma_start(mask_words[:, :], mask_rows[0:1, :].broadcast_to([P, N // 4])).then_inc(mask_in, 16)
                    act.dma_start(row_sb[:, :], rows.broadcast_to([P, 2 * DIM + DH])).then_inc(rows_in, 16)
                    for n, (lo, hi) in enumerate(BIAS_HEADS):
                        act.dma_start(bias[:, lo:hi, :], bias_rows[:, lo:hi, :]).then_inc(bias_in[n], 16)
                    act.wait_ge(cols_in, 16)
                    act.wait_ge(wkv_in, 16)
                    for kd in range(KD):
                        scale = gin_col[:, kd:kd + 1]
                        for half in range(2):
                            a.activation(wk_h[:, kd, DH * half:DH * (half + 1)], wkv_raw[:, kd, 0:DH],
                                         ACT.Identity, scale=scale)
                        i = a.activation(wv_h[:, kd, :], wkv_raw[:, kd, DH:2 * DH], ACT.Identity, scale=scale)
                    i.then_inc(wkv_hi, 1)
                    a.activation(k_sb[:, 0:1], nk_col[:, :], ACT.Copy).then_inc(nk_done, 1)
                    split_chunk(0)
                    split_chunk(1)
                    high("X", 0, b)
                    high("KV", 0, b)
                    for j in range(4):
                        high("Q", j, b)
                    return
                for p in range(PAIRS):
                    late = FILL_B.get((p - 1) % PAIRS, [])
                    early = FILL_A.get(p, [])
                    bb = b if p > 0 else b - 1
                    for n in late:
                        kind, j = JOBS[n]
                        if runs(kind, bb) and kind in ("X", "Q", "KV", "HT") and not (
                                isinstance(bb, int) and bb == -1):
                            high(kind, j, bb)
                        if kind == "F1" and runs(kind, bb):
                            hidden(j, bb)
                    if p != 3 and pair_runs(b, p - 3):
                        o_high(b, p - 3)
                    if attends(b):
                        exponentials(b, p)
                    if p == 3 and pair_runs(b, 0):
                        o_high(b, 0)
                    for n in late:
                        kind, j = JOBS[n]
                        if kind == "F1" and runs(kind, bb):
                            hidden_high(j, bb)
                    for n in early:
                        kind, j = JOBS[n]
                        if runs(kind, b) and kind in ("X", "Q", "KV", "HT"):
                            high(kind, j, b)
                        if kind == "F1" and runs(kind, b):
                            hidden(j, b)
                    if pair_runs(b, p - 1):
                        even_transposed(b, p - 1)
                    if attends(b):
                        normalise_even(b, p)
                    for n in early:
                        kind, j = JOBS[n]
                        if kind == "F1" and runs(kind, b):
                            hidden_high(j, b)
                    if isinstance(b, int) and b == 0 and p < 6:
                        split_chunk(p + 2)

            batches(act, batch)

        @block.vector
        def _(dve):
            v = nc.vector

            def low(kind, j, b):
                bank = G_ps[JOBS.index((kind, j)) % G_BANKS]
                if kind == "X":
                    dve.wait_ge(xT_hi, b + 2)
                    v.tensor_tensor(xT_l[:, :, :].rearrange("p a n -> p (a n)"), bank[:, :],
                                    view(xT_h[:, :, :]).rearrange("p a n -> p (a n)"),
                                    ALU.subtract).then_inc(xT_split, 1)
                elif kind == "HT":
                    dve.wait_ge(hT_hi, b)
                    v.tensor_tensor(hT_l[:, :, :].rearrange("p a n -> p (a n)"), bank[:, :],
                                    view(hT_h[:, :, :]).rearrange("p a n -> p (a n)"),
                                    ALU.subtract).then_inc(hT_split, 1)
                elif kind == "KV":
                    dve.wait_ge(k_ready, b + 2)
                    if not (isinstance(b, int) and b == -1):
                        dve.wait_ge(v_ready, b + 1)
                    for t in range(TT):
                        i = v.tensor_tensor(v_next[:, t, :], bank[:, N + t * DH:N + (t + 1) * DH],
                                            nv_row[:, :], ALU.subtract)
                    i.then_inc(kv_ready, 1)
                elif kind == "W":
                    attention_stats(j, b)
                elif kind == "F1":
                    n = 4 * (b - 1) + j
                    if j < 2 and isinstance(b, int) and b == 1:
                        if j == 0:
                            dve.wait_ge(b1_done, 1)
                            dve.wait_ge(chunk_done, 8)
                    else:
                        dve.wait_ge(y_ready, n - 1)
                    dve.wait_ge(full["F1"], n + 1)
                    v.tensor_tensor(u_buf[:, j % 2], bank[:, :].rearrange("p (m n) -> p m n", m=2),
                                    b1_col[:, 2 * j:2 * j + 2].unsqueeze(2).broadcast_to([P, 2, N]),
                                    ALU.add).then_inc(u_ready, 1)
                elif kind == "F2":
                    n = TT * (b - 2) + j
                    dve.wait_ge(base_ready, n + 1)
                    if not (isinstance(b, int) and b == 2):
                        dve.wait_ge(out_sent, 16 * TT * (b - 2))
                    dve.wait_ge(full["F2"], n + 1)
                    v.tensor_tensor(out_sb[:, j, :], bank[:, 0:DIM], base[:, j, :], ALU.add
                                    ).then_inc(out_ready, 1)

            def hidden_value(j, b):
                n = 4 * (b - 1) + j
                dve.wait_ge(tanh_done, n + 1)
                v.scalar_tensor_tensor(out=t_buf[:, j % 2], in0=t_buf[:, j % 2], scalar=1.0,
                                       in1=u_buf[:, j % 2], op0=ALU.add, op1=ALU.mult).then_inc(y_ready, 1)

            def aggregate(st, mv, var, t, stats, aggr, vare, n):
                dve.wait_ge(stats, n)
                gate(dve, dve_passed)
                v.bn_aggr(mv[:, t, :], st[:, t, :]).then_inc(aggr, 1)
                dve.wait_ge(aggr, n)
                v.tensor_scalar(var[:, t:t + 1], mv[:, t, 1:2], EPS, None, ALU.add).then_inc(vare, 1)

            def attention_stats(t, b):
                n = TT * (b - 1) + t + 1
                bank = G_ps[JOBS.index(("W", t)) % G_BANKS]
                dve.wait_ge(full["W"], n)
                v.bn_stats(a_st[:, t, :], bank[:, 0:DIM]).then_inc(a_stats, 1)
                aggregate(a_st, a_mv, a_var, t, a_stats, a_aggr, a_vare, n)

            def attention_norm(t, b):
                n = TT * (b - 1) + t + 1
                bank = G_ps[JOBS.index(("W", t)) % G_BANKS]
                dve.wait_ge(a_rstd, n)
                if t == 0:
                    if not (isinstance(b, int) and b == 1):
                        dve.wait_ge(base_ready, TT * (b - 1))
                    else:
                        dve.wait_ge(chunk_done, 8)
                v.tensor_scalar(hid[:, t, :], bank[:, 0:DIM], a_mv[:, t, 0:1], a_rs[:, t:t + 1],
                                ALU.subtract, ALU.mult).then_inc(a_normed, 1)

            def h_statistics(t, b):
                n = TT * (b - 1) + t + 1
                dve.wait_ge(h_ready, n)
                v.bn_stats(h_st[:, t, :], hid[:, t, :]).then_inc(h_stats, 1)
                aggregate(h_st, h_mv, h_var, t, h_stats, h_aggr, h_vare, n)

            def h_norm(t, b):
                n = TT * (b - 1) + t + 1
                dve.wait_ge(h_rstd, n)
                if t == 0 and not (isinstance(b, int) and b == 1):
                    dve.wait_ge(full["HT"], b - 1)
                v.tensor_scalar(hn[:, t, :], hid[:, t, :], h_mv[:, t, 0:1], h_rs[:, t:t + 1],
                                ALU.subtract, ALU.mult).then_inc(hn_ready, 1)

            def x_statistics(b):
                dve.wait_ge(x_in, 16 * (b + 2))
                for t in range(TT):
                    v.bn_stats(x_st[:, t, :], xs[:, t, :]).then_inc(x_stats, 1)
                dve.wait_ge(x_stats, TT * (b + 2))
                gate(dve, dve_passed)
                for t in range(TT):
                    v.bn_aggr(x_mv[:, t, :], x_st[:, t, :]).then_inc(x_aggr, 1)
                dve.wait_ge(x_aggr, TT * (b + 2))
                v.tensor_scalar(x_var[:, :], x_mv[:, :, 1], EPS, None, ALU.add).then_inc(x_vare, 1)

            def x_norm(b):
                dve.wait_ge(x_rstd, b + 2)
                if not (isinstance(b, int) and b == -1):
                    dve.wait_ge(full["X"], b + 1)
                for t in range(TT):
                    i = v.tensor_scalar(xn[:, t, :], xs[:, t, :], x_mv[:, t, 0:1], x_rs[:, t:t + 1],
                                        ALU.subtract, ALU.mult)
                i.then_inc(xn_ready, 1)

            def shift(b, p):
                n = PAIRS * b + p
                dve.wait_ge(scores_done, n + 1)
                for i in range(2):
                    s = (2 * p + i) % RING
                    dve.wait_ge(score_bias, 2 * n + i + 1)
                    gate(dve, dve_passed)
                    for qt, (c, w) in enumerate(((0, C0), (C0, C1))):
                        v.tensor_tensor_reduce(
                            out=score[:, s, c:c + w], in0=S_ps[i][:, c:c + w], in1=score[:, s, c:c + w],
                            scale=1.0, scalar=3.0e38, op0=ALU.add, op1=ALU.min,
                            accum_out=neg_max[:, s, qt:qt + 1]).then_inc(shifted, 1)

            def denominators(b, p):
                s = (2 * p) % RING
                dve.wait_ge(exp_done, 4 * (PAIRS * b + p + 1))
                v.reciprocal(rdenom[:, s:s + 2, :], denom[:, s:s + 2, :]).then_inc(rdenom_done, 1)

            def normalise_odd(b, p):
                s = (2 * p + 1) % RING
                dve.wait_ge(rdenom_done, PAIRS * b + p + 1)
                for qt, (c, w) in enumerate(((1, P), (C0 + 1, N))):
                    i = v.tensor_scalar(score[:, s, c:c + w], score[:, s, c:c + w],
                                        rdenom[:, s, qt:qt + 1], None, ALU.mult)
                i.then_inc(odd_done, 1)

            def odd_transposed(b, p):
                n = PAIRS * b + p
                dve.wait_ge(trans_done, n + 1)
                if not (isinstance(b, int) and n < 2):
                    dve.wait_ge(pv_done, n - 1)
                v.tensor_copy(pT[:, 2 * (p % 2) + 1, :], T_ps[1][:, 0:N + P]).then_inc(pT_odd, 1)

            def o_low(b, p):
                n = PAIRS * b + p
                dve.wait_ge(o_hi, n + 1)
                v.scalar_tensor_tensor(out=o_l[:, p % PAIRS, :], in0=O_ps[:, 0:N], scalar=nv_col[:, :],
                                       in1=view(o_h[:, p % PAIRS, :]), op0=ALU.add,
                                       op1=ALU.subtract).then_inc(o_split, 1)

            def take_values(b):
                if not (isinstance(b, int) and b == 0):
                    dve.wait_ge(pv_done, PAIRS * b)
                dve.wait_ge(kv_ready, b + 1)
                v.tensor_copy(v_live[:, :, :], v_next[:, :, :]).then_inc(v_ready, 1)

            def dequantise(c):
                dve.wait_ge(stage_in[c % 2], 32 + 32 * ((c - 4) // 2 + 1))
                v.scalar_tensor_tensor(out=w_raw[c % 2], in0=w_raw[c % 2].bitcast(I32), scalar=-128.0,
                                       in1=s_raw[c % 2], op0=ALU.add, op1=ALU.mult).then_inc(chunk_deq, 1)

            def split_chunk(c):
                hi, lo = chunk_dst(c)
                dve.wait_ge(chunk_hi, c + 1)
                v.scalar_tensor_tensor(out=lo, in0=w_raw[c % 2], scalar=chunk_scale(c), in1=view(hi),
                                       op0=ALU.mult, op1=ALU.subtract).then_inc(chunk_done, 1)

            def batch(b):
                if isinstance(b, int) and b == -1:
                    x_statistics(b)
                    dve.wait_ge(cols_in, 16)
                    dve.wait_ge(wkv_hi, 1)
                    for kd in range(KD):
                        scale = gin_col[:, kd:kd + 1]
                        for half in range(2):
                            s = slice(DH * half, DH * (half + 1))
                            v.scalar_tensor_tensor(out=wk_l[:, kd, s], in0=wkv_raw[:, kd, 0:DH], scalar=scale,
                                                   in1=view(wk_h[:, kd, s]), op0=ALU.mult, op1=ALU.subtract)
                        i = v.scalar_tensor_tensor(out=wv_l[:, kd, :], in0=wkv_raw[:, kd, DH:2 * DH],
                                                   scalar=scale, in1=view(wv_h[:, kd, :]), op0=ALU.mult,
                                                   op1=ALU.subtract)
                    i.then_inc(wkv_done, 1)
                    x_norm(b)
                    split_chunk(0)
                    split_chunk(1)
                    dve.wait_ge(rows_in, 16)
                    v.tensor_scalar(b2_row[:, :], b2_row[:, :], 0.5, None, ALU.mult).then_inc(b2_half, 1)
                    low("X", 0, b)
                    low("KV", 0, b)
                    return
                for p in range(PAIRS):
                    late = FILL_B.get((p - 1) % PAIRS, [])
                    early = FILL_A.get(p, [])
                    bb = b if p > 0 else b - 1
                    if isinstance(bb, int) and bb == -1:
                        late = []
                    if p == 1 and inside(b, 0, B - 2):
                        x_norm(b)
                    if p == 2 and attends(b):
                        take_values(b)
                    if inside(b, 1, B):
                        if p == 3:
                            attention_norm(0, b)
                        if p == 4:
                            attention_norm(1, b)
                        if p == 5:
                            h_norm(0, b)
                            h_norm(1, b)
                    for n in late:
                        if runs(JOBS[n][0], bb):
                            low(*JOBS[n], bb)
                    if p != 3 and pair_runs(b, p - 3):
                        o_low(b, p - 3)
                    if attends(b):
                        shift(b, p)
                    for n in late:
                        if JOBS[n][0] == "F1" and runs("F1", bb):
                            hidden_value(JOBS[n][1], bb)
                    if p == 3 and pair_runs(b, 0):
                        o_low(b, 0)
                    for n in early:
                        if runs(JOBS[n][0], b):
                            low(*JOBS[n], b)
                    if p == 0 and inside(b, 0, B - 2):
                        x_statistics(b)
                    if inside(b, 1, B):
                        if p == 3:
                            h_statistics(0, b)
                        if p == 4:
                            h_statistics(1, b)
                    if pair_runs(b, p - 1):
                        odd_transposed(b, p - 1)
                    if attends(b):
                        denominators(b, p)
                        normalise_odd(b, p)
                    for n in early:
                        if JOBS[n][0] == "F1" and runs("F1", b):
                            hidden_value(JOBS[n][1], b)
                    if isinstance(b, int) and b == 0:
                        if p == 2:
                            dequantise(4)
                            dequantise(5)
                        if p in (4, 5):
                            dequantise(p + 2)
                        if p < 6:
                            split_chunk(p + 2)
                        if p == 3:
                            dve.wait_ge(full["BT"], 1)
                            v.tensor_tensor(b1_col[:, :], G_ps[7 % G_BANKS][:, 0:FM], b1_col[:, :],
                                            ALU.add).then_inc(b1_done, 1)

            batches(dve, batch)

        @block.tensor
        def _(pe):
            mm = nc.tensor.matmul

            def three(dst, lhs_h, lhs_l, rhs_h, rhs_l, first, last):
                mm(dst, lhs_h, rhs_h, start=first, stop=False)
                mm(dst, lhs_h, rhs_l, start=False, stop=False)
                return mm(dst, lhs_l, rhs_h, start=False, stop=last)

            def job(i, b):
                kind, j = JOBS[i]
                bank = G_ps[i % G_BANKS]
                before = bank_before(i, b)
                if before:
                    pe.wait_ge(emptied[before[0]], before[1])
                if kind == "X":
                    pe.wait_ge(xn_ready, b + 2)
                    for kd in range(KD):
                        for t in range(TT):
                            last = nc.tensor.transpose(bank[:, kd * N + t * P:kd * N + (t + 1) * P],
                                                       xn[:, t, kd * P:(kd + 1) * P], ident[:, :])
                elif kind == "HT":
                    pe.wait_ge(hn_ready, TT * b)
                    for kd in range(KD):
                        for t in range(TT):
                            last = nc.tensor.transpose(bank[:, kd * N + t * P:kd * N + (t + 1) * P],
                                                       hn[:, t, kd * P:(kd + 1) * P], ident[:, :])
                elif kind == "Q":
                    pe.wait_ge(xT_split, b + 2)
                    for m in range(2):
                        cols = slice((2 * j + m) * P, (2 * j + m + 1) * P)
                        for kd in range(KD):
                            last = three(bank[:, m * N:(m + 1) * N], wq_h[:, kd, cols], wq_l[:, kd, cols],
                                         xT_h[:, kd, :], xT_l[:, kd, :], kd == 0, kd == KD - 1)
                elif kind == "KV":
                    pe.wait_ge(xT_split, b + 2)
                    for kd in range(KD):
                        three(bank[:, 0:N], wk_h[:, kd, :], wk_l[:, kd, :], xT_h[:, kd, :], xT_l[:, kd, :],
                              kd == 0, kd == KD - 1)
                    for t in range(TT):
                        rows = slice(t * P, (t + 1) * P)
                        for kd in range(KD):
                            last = three(bank[:, N + t * DH:N + (t + 1) * DH], xT_h[:, kd, rows],
                                         xT_l[:, kd, rows], wv_h[:, kd, :], wv_l[:, kd, :],
                                         kd == 0, kd == KD - 1)
                elif kind == "W":
                    pe.wait_ge(o_split, PAIRS * b)
                    rows = slice(j * P, (j + 1) * P)
                    for p in range(PAIRS):
                        last = three(bank[:, 0:DIM], o_h[:, p, rows], o_l[:, p, rows], wo_h[:, p, :],
                                     wo_l[:, p, :], p == 0, p == PAIRS - 1)
                elif kind == "F1":
                    pe.wait_ge(hT_split, b)
                    for m in range(2):
                        cols = slice((2 * j + m) * P, (2 * j + m + 1) * P)
                        for kd in range(KD):
                            last = three(bank[:, m * N:(m + 1) * N], w1_h[:, kd, cols], w1_l[:, kd, cols],
                                         hT_h[:, kd, :], hT_l[:, kd, :], kd == 0, kd == KD - 1)
                elif kind == "F2":
                    pe.wait_ge(y_split, 4 * (b - 1))
                    rows = slice(j * P, (j + 1) * P)
                    for m in range(FM):
                        last = three(bank[:, 0:DIM], y_h[:, m, rows], y_l[:, m, rows], w2_h[:, m, :],
                                     w2_l[:, m, :], m == 0, m == FM - 1)
                last.then_inc(full[kind], 1)

            def scores(b, p):
                n = PAIRS * b + p
                if not (isinstance(b, int) and n == 0):
                    pe.wait_ge(shifted, 4 * n)
                if p % 2 == 0:
                    pe.wait_ge(q_ready, 4 * b + p // 2 + 1)
                if p == 0:
                    pe.wait_ge(k_ready, b + 1)
                for qt, (a, w) in enumerate(((0, C0), (C0, C1))):
                    for i in range(2):
                        r = slice(DH * i, DH * (i + 1))
                        last = mm(S_ps[i][:, a:a + w], q_sb[r, p, qt * P:(qt + 1) * P], k_sb[r, 0:w],
                                  start=True, stop=True)
                last.then_inc(scores_done, 1)

            def transposes(b, p):
                n = PAIRS * b + p
                if not (isinstance(b, int) and n == 0):
                    pe.wait_ge(pT_even, n)
                    pe.wait_ge(pT_odd, n)
                pe.wait_ge(even_done, n + 1)
                pe.wait_ge(odd_done, n + 1)
                for i in range(2):
                    s = (2 * p + i) % RING
                    for c, a in enumerate((1, C0 + 1, C0 + 1 + P)):
                        last = nc.tensor.transpose(T_ps[i][:, c * P:(c + 1) * P], score[:, s, a:a + P],
                                                   ident[:, :])
                last.then_inc(trans_done, 1)

            def values(b, p):
                n = PAIRS * b + p
                if not (isinstance(b, int) and n == 0):
                    pe.wait_ge(o_split, n)
                if p % PAIRS == 0:
                    pe.wait_ge(v_ready, b + 1)
                pe.wait_ge(pT_even, n + 1)
                pe.wait_ge(pT_odd, n + 1)
                gate(pe, pe_passed)
                for kt in range(2):
                    for i in range(2):
                        last = mm(O_ps[DH * i:DH * (i + 1), kt * P:N], v_live[:, kt, :],
                                  pT[:, 2 * (p % 2) + i, kt * N:N + kt * P], start=kt == 0, stop=kt == 1)
                last.then_inc(pv_done, 1)

            def shift_product():
                before = bank_before(7, 0)
                pe.wait_ge(emptied[before[0]], before[1])
                pe.wait_ge(chunk_deq, 2)
                for m in range(FM):
                    for kd in range(KD):
                        last = mm(G_ps[7 % G_BANKS][:, m:m + 1], w_raw[kd][:, m * P:(m + 1) * P],
                                  bet_col[:, kd:kd + 1], start=kd == 0, stop=kd == KD - 1)
                last.then_inc(full["BT"], 1)

            def batch(b):
                if isinstance(b, int) and b == -1:
                    pe.wait_ge(ident_done, 1)
                    job(3, b)
                    pe.wait_ge(wkv_done, 1)
                    job(13, b)
                    pe.wait_ge(nk_done, 1)
                    pe.wait_ge(chunk_done, 2)
                    for i in (5, 6, 12, 14):
                        job(i, b)
                    return
                for p in range(PAIRS):
                    if attends(b):
                        scores(b, p)
                    for i in FILL_A.get(p, []):
                        if runs(JOBS[i][0], b):
                            job(i, b)
                    if isinstance(b, int) and b == 0 and p == 3:
                        shift_product()
                    if pair_runs(b, p - 1):
                        transposes(b, p - 1)
                    for i in FILL_B.get(p, []):
                        if runs(JOBS[i][0], b):
                            job(i, b)
                    if pair_runs(b, p - 2):
                        values(b, p - 2)

            batches(pe, batch)


def kernel(**inputs):
    import numpy as np
    import concourse.bacc as bacc
    from concourse.bass_utils import run_bass_kernel_spmd

    def col(a):
        return np.reshape(a, (-1, P)).T

    v = {n.removeprefix("L0_"): np.asarray(a) for n, a in inputs.items()}
    null_k, null_v = v["cond_64"][0], v["cond_64"][1]
    bias, null = v["fside_16xSxS_0"], v["cond_null_attn_bias"]
    null = np.broadcast_to(null[None, :, None], (P, H, 1))
    arrays = {
        "x": v["x"],
        "bias_rows": np.concatenate([null, bias[:, :P, :P].transpose(1, 0, 2),
                                     null, bias[:, P:, :].transpose(1, 0, 2)], axis=2),
        "mask_rows": np.ascontiguousarray(v["mask_BxS_bk0"]).view(np.int32),
        "wq": v["cond_Wq"], "wkv": v["cond_Wkv"], "wo": v["cond_Wo"],
        "q1": v["ffn_fc1_q"], "s1": v["ffn_fc1_scales"],
        "q2": v["ffn_fc2_q"], "s2": v["ffn_fc2_scales"],
        "columns": np.concatenate([col(v["cond_g_in"]), col(v["ffn_ln_gamma"]), col(v["ffn_ln_beta"]),
                                   col(v["ffn_fc1_bias"]), col(np.tile(null_k, 2)),
                                   col(np.tile(null_v, 2))], axis=1),
        "rows": np.concatenate([v["cond_g_out"], v["ffn_fc2_bias"], null_v])[None, :],
    }
    nc = bacc.Bacc("TRN2", target_bir_lowering=False, num_devices=1)
    arrays = {n: np.ascontiguousarray(a) for n, a in arrays.items()}
    args = {n: nc.dram_tensor(f"in_{n}", a.shape, mybir.dt.from_np(a.dtype), kind="ExternalInput").ap()
            for n, a in arrays.items()}
    out = nc.dram_tensor("out_rows", (B, N, DIM), F32, kind="ExternalOutput").ap()
    build(nc, **args, out=out)
    r = run_bass_kernel_spmd(nc, [{f"in_{n}": a for n, a in arrays.items()}], core_ids=[0])
    return r.results[0]["out_rows"]
```

```python
from contextlib import ExitStack

import concourse.bass as bass
from concourse import mybir

ALU = mybir.AluOpType
ACT = mybir.ActivationFunctionType
F32 = mybir.dt.float32
F32R = mybir.dt.float32r
I32 = mybir.dt.int32
U8 = mybir.dt.uint8

P = 128
B, N, DIM = 8, 256, 256
H, DH = 16, 64
INNER = H * DH
F = 1024
EPS = 1e-5
BIG = 1.0e38
PAIRS = H // 2
KD = DIM // P
TT = N // P
FM = F // P
C0 = 1 + P
C1 = 1 + N
CS = C0 + C1
RING = 8

JOBS = [("F1", 2), ("Q", 3), ("F1", 3), ("X", 0), ("W", 0), ("Q", 0), ("W", 1), ("F2", 0), ("Q", 1),
        ("F2", 1), ("HT", 0), ("F1", 0), ("Q", 2), ("KV", 0), ("F1", 1)]
PER = {"F2": 2, "W": 2, "X": 1, "Q": 4, "HT": 1, "F1": 4, "KV": 1, "BT": 1}
LAG = {"F2": 2, "W": 1, "HT": 1, "F1": 1, "X": -1, "Q": -1, "KV": -1}
LATER = [("F1", 2), ("F1", 3), ("Q", 3)]
FILL_A = {0: [("F1", 2)], 1: [("F1", 3)], 2: [("W", 0)], 3: [("W", 1)], 4: [("F2", 0)],
          5: [("F2", 1), ("HT", 0)], 6: [("F1", 0)], 7: [("KV", 0)]}
FILL_B = {0: [("Q", 3)], 1: [("X", 0)], 2: [("Q", 0)], 4: [("Q", 1)], 6: [("Q", 2)], 7: [("F1", 1)]}
FIRST_QUERIES = {0: 1, 1: 2, 2: 3}
G_BANKS = 3
WARM_UP = (20, 12)
CHUNK_HIGH = {(0, 0): [2], (0, 1): [3], (0, 3): [4], (0, 4): [5], (0, 6): [6], (0, 7): [7]}
CHUNK_DEQUANTISE = {(0, 2): [4], (0, 3): [5], (0, 5): [6], (0, 6): [7]}
W1_LOW = {(0, 3): [4], (0, 4): [5]}
CHUNK_LOW = {(0, 0): [2], (0, 1): [3], (0, 7): [6], (1, 0): [7]}
SHIFT_STEP = 4
SHIFT_COLS = 512 // FM
SHIFT_SLOT = ("W", 1)


def bank_of(kind, j):
    return JOBS.index((kind, j)) % G_BANKS


def lag(kind, j):
    return LAG[kind] + ((kind, j) in LATER)


def runs(kind, j, b):
    return not isinstance(b, int) or 0 <= b - lag(kind, j) < B


def count(kind, j, b):
    return PER[kind] * (b - lag(kind, j)) + j + 1


def bank_before(kind, j, b):
    i = JOBS.index((kind, j))
    while True:
        i -= G_BANKS
        if i < 0:
            i += len(JOBS)
            b = b - 1
            if isinstance(b, int) and b < -1:
                return None
        kind, j = JOBS[i]
        if isinstance(b, int) and b == 0 and (kind, j) == SHIFT_SLOT:
            return "BT", 1
        if runs(kind, j, b):
            return kind, count(kind, j, b)


def build(nc, x, bias_rows, mask_rows, wq, wkv, wo, q1, s1, q2, s2, columns, rows, out):
    with ExitStack() as ctx:
        def sb(name, shape, dt=F32):
            return ctx.enter_context(nc.sbuf_tensor(name, shape, dt))

        def psum(name, shape, dt=F32):
            return ctx.enter_context(nc.psum_tensor(name, shape, dt))

        def sem(name):
            return ctx.enter_context(nc.semaphore(name))

        wq_h, wq_l = sb("wq_h", [P, KD, INNER], F32R), sb("wq_l", [P, KD, INNER], F32R)
        wkv_h, wkv_l = sb("wkv_h", [P, KD, 3 * DH], F32R), sb("wkv_l", [P, KD, 3 * DH], F32R)
        wk_h, wk_l, wv_h, wv_l = (wkv_h[:, :, 0:P], wkv_l[:, :, 0:P], wkv_h[:, :, P:], wkv_l[:, :, P:])
        wo_h, wo_l = sb("wo_h", [P, PAIRS, DIM], F32R), sb("wo_l", [P, PAIRS, DIM], F32R)
        w1_h, w1_l = sb("w1_h", [P, KD, F], F32R), sb("w1_l", [P, KD, F], F32R)
        w2_h, w2_l = sb("w2_h", [P, FM, DIM], F32R), sb("w2_l", [P, FM, DIM], F32R)
        xT_h, xT_l = sb("xT_h", [P, KD, N], F32R), sb("xT_l", [P, KD, N], F32R)
        hT_h, hT_l = sb("hT_h", [P, KD, N], F32R), sb("hT_l", [P, KD, N], F32R)
        q_sb, k_sb = sb("q_sb", [P, PAIRS, N]), sb("k_sb", [P, 1 + N])
        o_h, o_l = sb("o_h", [P, PAIRS, N], F32R), sb("o_l", [P, PAIRS, N], F32R)
        y_h, y_l = sb("y_h", [P, FM, N], F32R), sb("y_l", [P, FM, N], F32R)
        bias = sb("bias", [P, H, CS])
        maskrow = sb("maskrow", [P, CS])
        mask_words = sb("mask_words", [P, N // 4], I32)
        score = sb("score", [P, RING, CS])
        neg_max = sb("neg_max", [P, RING, 2])
        denom = sb("denom", [P, RING, 2])
        rdenom = sb("rdenom", [P, RING, 2])
        pT = sb("pT", [P, 4, N + P])
        v_next = sb("v_next", [P, TT, DH])
        v_live = sb("v_live", [P, TT, DH])
        xs = sb("xs", [P, TT, DIM])
        xn = sb("xn", [P, TT, DIM])
        scratch = sb("scratch", [P, 16, DIM])
        u_buf = scratch[:, 0:4, :].rearrange("p (r m) n -> p r m n", r=2)
        t_buf = scratch[:, 4:8, :].rearrange("p (r m) n -> p r m n", r=2)
        hid = scratch[:, 8:10, :]
        hn = scratch[:, 10:12, :]
        base = scratch[:, 12:14, :]
        xres = scratch[:, 14:16, :]
        w_raw = [scratch[:, 4 * i:4 * i + 4, :].rearrange("p a n -> p (a n)") for i in range(2)]
        s_raw = [scratch[:, 8 + 4 * i:12 + 4 * i, :].rearrange("p a n -> p (a n)") for i in range(2)]
        out_sb = sb("out_sb", [P, TT, DIM])
        row_sb = sb("row_sb", [P, 2 * DIM + DH])
        gout_row, b2_row, nv_row = (row_sb[:, 0:DIM], row_sb[:, DIM:2 * DIM],
                                    row_sb[:, 2 * DIM:2 * DIM + DH])
        wkv_raw = sb("wkv_raw", [P, KD, 3 * DH])
        col_sb = sb("col_sb", [P, 3 * KD + FM + 2])
        gin_col, gam_col, bet_col = (col_sb[:, KD * i:KD * (i + 1)] for i in range(3))
        b1_col = col_sb[:, 3 * KD:3 * KD + FM]
        nk_col, nv_col = (col_sb[:, 3 * KD + FM + i:3 * KD + FM + i + 1] for i in range(2))
        ident = sb("ident", [P, P])
        halves = sb("halves", [P, TT])
        x_st, x_mv, x_var, x_rs = (sb("x_st", [P, TT, 6]), sb("x_mv", [P, TT, 2]),
                                   sb("x_var", [P, TT]), sb("x_rs", [P, TT]))
        a_st, a_mv, a_var, a_rs = (sb("a_st", [P, TT, 6]), sb("a_mv", [P, TT, 2]),
                                   sb("a_var", [P, TT]), sb("a_rs", [P, TT]))
        h_st, h_mv, h_var, h_rs = (sb("h_st", [P, TT, 6]), sb("h_mv", [P, TT, 2]),
                                   sb("h_var", [P, TT]), sb("h_rs", [P, TT]))

        S_ps = [psum(f"S_ps{i}", [P, 512]) for i in range(2)]
        T_ps = [psum(f"T_ps{i}", [P, 512]) for i in range(2)]
        O_ps = psum("O_ps", [P, 512])
        G_ps = [psum(f"G_ps{i}", [P, 512]) for i in range(G_BANKS)]

        def view(t):
            return t.bitcast(F32)

        x_in, xres_in, mask_in = sem("x_in"), sem("xres_in"), sem("mask_in")
        cols_in, wkv_in, wq_in = sem("cols_in"), sem("wkv_in"), [sem("wq_in0"), sem("wq_in1")]
        rows_in = sem("rows_in")
        stage_in = [sem("stage_in0"), sem("stage_in1")]
        bias_in = [sem(f"bias_in{i}") for i in range(4)]
        out_sent = sem("out_sent")
        wkv_hi, wkv_done = sem("wkv_hi"), sem("wkv_done")
        chunk_deq, chunk_hi = sem("chunk_deq"), sem("chunk_hi")
        half_done = [sem("half_done0"), sem("half_done1")]
        ident_zero, ident_done, nk_done = sem("ident_zero"), sem("ident_done"), sem("nk_done")
        causal_done, halves_done, mask_edge = sem("causal_done"), sem("halves_done"), sem("mask_edge")
        b2_half, b1_done = sem("b2_half"), sem("b1_done")
        mask_ready, score_bias = sem("mask_ready"), sem("score_bias")
        scores_done, shifted, exp_done = sem("scores_done"), sem("shifted"), sem("exp_done")
        rdenom_done, even_done, odd_done, trans_done = (
            sem("rdenom_done"), sem("even_done"), sem("odd_done"), sem("trans_done"))
        pT_even, pT_odd, pv_done = sem("pT_even"), sem("pT_odd"), sem("pv_done")
        o_hi, o_split, v_ready = sem("o_hi"), sem("o_split"), sem("v_ready")
        full = {k: sem(f"{k}_full") for k in ("F2", "W", "X", "Q", "HT", "F1", "KV", "BT")}
        xT_hi, hT_hi, k_ready = sem("xT_hi"), sem("hT_hi"), sem("k_ready")
        q_ready, kv_ready, xT_split, hT_split = (
            sem("q_ready"), sem("kv_ready"), sem("xT_split"), sem("hT_split"))
        a_normed, u_ready, out_ready = sem("a_normed"), sem("u_ready"), sem("out_ready")
        emptied = {"F2": out_ready, "W": a_normed, "X": xT_split, "Q": q_ready, "HT": hT_split,
                   "F1": u_ready, "KV": kv_ready, "BT": b1_done}
        x_stats, x_aggr, x_vare, x_rstd, xn_ready = (
            sem("x_stats"), sem("x_aggr"), sem("x_vare"), sem("x_rstd"), sem("xn_ready"))
        a_stats, a_aggr, a_vare, a_rstd = sem("a_stats"), sem("a_aggr"), sem("a_vare"), sem("a_rstd")
        h_ready, base_x, base_ready = sem("h_ready"), sem("base_x"), sem("base_ready")
        h_stats, h_aggr, h_vare, h_rstd, hn_ready = (
            sem("h_stats"), sem("h_aggr"), sem("h_vare"), sem("h_rstd"), sem("hn_ready"))
        tanh_done, y_ready, y_hi, y_split = (
            sem("tanh_done"), sem("y_ready"), sem("y_hi"), sem("y_split"))

        dve_passed, pool_passed, pe_passed = sem("dve_passed"), sem("pool_passed"), sem("pe_passed")

        block = ctx.enter_context(nc.Block())

        def batches(eng, batch):
            batch(-1)
            batch(0)
            batch(1)
            with eng.Fori(2, B - 1) as b:
                batch(b)
            batch(B - 1)
            batch(B)
            batch(B + 1)

        def inside(b, lo, hi):
            return not isinstance(b, int) or lo <= b <= hi

        def jobs_a(b, p):
            if isinstance(b, int) and b == 0 and p == 0:
                return [("Q", 1, -1)]
            if isinstance(b, int) and b == 0 and p in FIRST_QUERIES:
                return [("Q", 3, 0), ("X", 0, 0)] if p == 2 else [("Q", 2, -1)]
            return [(kind, j, b) for kind, j in FILL_A.get(p, []) if runs(kind, j, b)]

        def jobs_b(b, p):
            if p < 0:
                b, p = b - 1, p + PAIRS
                if isinstance(b, int) and b < 0:
                    return []
            if isinstance(b, int) and b == 0 and p < 4:
                return [("Q", 0, 0)] if p == 3 else []
            return [(kind, j, b) for kind, j in FILL_B.get(p, []) if runs(kind, j, b)]

        def attends(b):
            return inside(b, 0, B - 1)

        def pair_runs(b, p):
            return not isinstance(b, int) or 0 <= PAIRS * b + p < PAIRS * B

        def gate(eng, passed):
            eng.sem_inc(passed, 1)

        def chunk_src(c):
            if c < 2:
                r = wq.rearrange("(a p) n -> p a n", p=P)
                return r[:, :, c * INNER // 2:(c + 1) * INNER // 2]
            if c < 4:
                r = wo.rearrange("(a p) n -> p a n", p=P)
                return r[:, 4 * (c - 2):4 * (c - 1), :]
            if c < 6:
                return q1[(c - 4) * P:(c - 3) * P, :]
            r = q2.rearrange("(a p) n -> p a n", p=P)
            return r[:, 4 * (c - 6):4 * (c - 5), :]

        def chunk_scales(c):
            if c < 6:
                return s1[c - 4:c - 3, :].broadcast_to([P, F])
            r = s2[4 * (c - 6):4 * (c - 5), :]
            return r.rearrange("(o g) n -> o g n", o=1).broadcast_to([P, 4, DIM])

        def chunk_dst(c):
            if c < 4:
                s = slice(4 * (c - 2), 4 * (c - 1))
                return (wo_h[:, s, :].rearrange("p a n -> p (a n)"),
                        wo_l[:, s, :].rearrange("p a n -> p (a n)"))
            if c < 6:
                return w1_h[:, c - 4, :], w1_l[:, c - 4, :]
            s = slice(4 * (c - 6), 4 * (c - 5))
            return (w2_h[:, s, :].rearrange("p a n -> p (a n)"),
                    w2_l[:, s, :].rearrange("p a n -> p (a n)"))

        def chunk_split(eng, c):
            eng.wait_ge(half_done[c % 2], c // 2 + 1)
            if c > 0:
                eng.wait_ge(half_done[(c - 1) % 2], (c - 1) // 2 + 1)

        BIAS_HEADS = [(0, 2), (2, 4), (4, 8), (8, 16)]

        @block.sync
        def _(sp):
            def load_x(b):
                rows = x[b] if isinstance(b, int) else x[bass.ds(b, 1)].rearrange("o r c -> (o r) c")
                sp.dma_start(xs[:, :, :], rows.rearrange("(t p) c -> p t c", p=P)).then_inc(x_in, 16)

            def load_mask(b):
                src = mask_rows[b:b + 1, :] if isinstance(b, int) else mask_rows[bass.ds(b, 1), :]
                sp.dma_start(mask_words[:, :], src.broadcast_to([P, N // 4])).then_inc(mask_in, 16)

            def load_chunk(c):
                if c >= 2:
                    sp.wait_ge(half_done[c % 2], c // 2)
                dst = w_raw[c % 2] if c < 4 else w_raw[c % 2].bitcast(I32)
                if c < 2:
                    dst = dst.rearrange("p (a n) -> p a n", a=2)
                if 2 <= c < 4 or c >= 6:
                    dst = dst.rearrange("p (a n) -> p a n", a=4)
                if c >= 6:
                    sp.wait_ge(full["BT"], 1)
                sp.dma_start(dst, chunk_src(c)).then_inc(stage_in[c % 2], 16)
                if c >= 4:
                    d = s_raw[c % 2]
                    if c >= 6:
                        d = d.rearrange("p (a n) -> p a n", a=4)
                    sp.dma_start(d, chunk_scales(c)).then_inc(stage_in[c % 2], 16)

            def batch(b):
                if isinstance(b, int) and b == -1:
                    load_x(0)
                    wkv_rows = wkv.rearrange("(a p) n -> p a n", p=P)
                    sp.dma_start(wkv_raw[:, :, DH:], wkv_rows).then_inc(wkv_in, 16)
                    sp.dma_start(wkv_raw[:, :, 0:DH], wkv_rows[:, :, 0:DH]).then_inc(wkv_in, 16)
                    load_chunk(0)
                    load_chunk(1)
                    sp.wait_ge(xn_ready, 1)
                    load_x(1)
                    sp.wait_ge(mask_ready, 1)
                    load_mask(1)
                    load_chunk(2)
                    load_chunk(3)
                    lo, hi = BIAS_HEADS[3]
                    sp.dma_start(bias[:, lo:hi, :], bias_rows[:, lo:hi, :]).then_inc(bias_in[3], 16)
                    for c in range(4, 8):
                        load_chunk(c)
                    return
                if inside(b, 1, B - 2):
                    sp.wait_ge(xn_ready, b + 1)
                    load_x(b + 1)
                if inside(b, 1, B):
                    if not (isinstance(b, int) and b == 1):
                        sp.wait_ge(base_x, TT * (b - 1))
                    else:
                        chunk_split(sp, 7)
                    rows = x[b - 1] if isinstance(b, int) else \
                        x[bass.ds(b - 1, 1)].rearrange("o r c -> (o r) c")
                    sp.dma_start(xres, rows.rearrange("(t p) c -> p t c", p=P)).then_inc(xres_in, 16)
                if inside(b, 1, B - 2):
                    sp.wait_ge(mask_ready, b + 1)
                    load_mask(b + 1)
                if inside(b, 2, B + 1):
                    for t in range(TT):
                        sp.wait_ge(out_ready, TT * (b - 2) + t + 1)
                        rows = out[b - 2] if isinstance(b, int) else \
                            out[bass.ds(b - 2, 1)].rearrange("o r c -> (o r) c")
                        sp.dma_start(rows[t * P:(t + 1) * P, :], out_sb[:, t, :]).then_inc(out_sent, 16)

            batches(sp, batch)
            sp.wait_ge(out_sent, 16 * B * TT)

        @block.gpsimd
        def _(pool):
            g = nc.gpsimd

            def convert_mask(b):
                pool.wait_ge(mask_in, 16 * (b + 1))
                if not isinstance(b, int) or b > 0:
                    pool.wait_ge(score_bias, H * b)
                    gate(pool, pool_passed)
                for a, w in ((1, P), (C0 + 1, N)):
                    i = g.tensor_scalar(maskrow[:, a:a + w], mask_words[:, :].bitcast(U8)[:, 0:w], -BIG, BIG, ALU.mult, ALU.add)
                i.then_inc(mask_ready, 1)

            def bias_scores(b, p):
                for i in range(2):
                    h = 2 * p + i
                    if isinstance(b, int) and b == 0:
                        group = [n for n, (lo, hi) in enumerate(BIAS_HEADS) if lo <= h < hi][0]
                        pool.wait_ge(bias_in[group], 16)
                        fresh = i == 0
                        if fresh:
                            for a in (1, C0 + 1 + P):
                                blk = bias[:, h:h + 2, a:a + P]
                                c = g.affine_select(out=blk, in_=blk, pattern=[[0, 2], [-1, P]],
                                                    compare_op=ALU.is_ge, fill=-BIG, base=0,
                                                    channel_multiplier=1)
                                c.then_inc(causal_done, 1)
                        pool.wait_ge(causal_done, 2 * (p + 1))
                    if not (isinstance(b, int) and b == 0 and h < RING):
                        pool.wait_ge(trans_done, PAIRS * b + p - RING // 2 + 1)
                    if i == 0:
                        pool.wait_ge(mask_ready, b + 1)
                    g.tensor_tensor(score[:, h % RING, :], maskrow[:, :], bias[:, h, :],
                                    ALU.subtract).then_inc(score_bias, 1)

            def power(out_, in_, n):
                return g.tensor_tensor(out_, in_, halves[:, 0:n], ALU.pow)

            def h_rows(b, t):
                pool.wait_ge(a_normed, TT * (b - 1) + t + 1)
                g.tensor_tensor(hid[:, t, :], hid[:, t, :], gout_row[:, :], ALU.mult).then_inc(h_ready, 1)

            def base_rows(b, t):
                if t == 0:
                    pool.wait_ge(xres_in, 16 * b)
                    if not (isinstance(b, int) and b < 2):
                        pool.wait_ge(out_ready, TT * (b - 1))
                    else:
                        pool.wait_ge(b2_half, 1)
                g.tensor_tensor(base[:, t, :], xres[:, t, :], b2_row[:, :], ALU.add).then_inc(base_x, 1)
                pool.wait_ge(base_x, TT * (b - 1) + t + 1)
                pool.wait_ge(h_ready, TT * (b - 1) + t + 1)
                g.tensor_tensor(base[:, t, :], base[:, t, :], hid[:, t, :], ALU.add).then_inc(base_ready, 1)

            def y_low(j, b):
                pool.wait_ge(y_hi, count("F1", j, b))
                g.tensor_tensor(y_l[:, 2 * j:2 * j + 2, :], t_buf[:, j % 2], view(y_h[:, 2 * j:2 * j + 2, :]),
                                ALU.subtract).then_inc(y_split, 1)

            def split_chunk(c):
                hi, lo = chunk_dst(c)
                pool.wait_ge(chunk_hi, c + 1)
                g.tensor_tensor(lo, w_raw[c % 2], view(hi), ALU.subtract).then_inc(half_done[c % 2], 1)

            def x_power(b):
                pool.wait_ge(x_vare, b + 2)
                power(x_rs[:, :], x_var[:, :], TT).then_inc(x_rstd, 1)

            def batch(b):
                if isinstance(b, int) and b == -1:
                    g.memset(halves[:, :], -0.5).then_inc(halves_done, 1)
                    g.memset(maskrow[:, 0:CS:C0], 0.0).then_inc(mask_edge, 1)
                    g.memset(ident[:, :], 0.0).then_inc(ident_zero, 1)
                    pool.wait_ge(ident_zero, 1)
                    g.affine_select(out=ident[:, :], in_=ident[:, :], compare_op=ALU.not_equal, fill=1.0,
                                    base=0, pattern=[[-1, P]], channel_multiplier=1).then_inc(ident_done, 1)
                    pool.wait_ge(halves_done, 1)
                    x_power(b)
                    pool.wait_ge(mask_edge, 1)
                    convert_mask(0)
                    bias_scores(0, 0)
                    return
                for p in range(PAIRS):
                    if attends(b):
                        if p < PAIRS - 1:
                            bias_scores(b, p + 1)
                        elif inside(b, 0, B - 2):
                            convert_mask(b + 1)
                            bias_scores(b + 1, 0)
                    if inside(b, 0, B - 2) and p == 0:
                        x_power(b)
                    if inside(b, 1, B):
                        if p == 2:
                            pool.wait_ge(a_vare, TT * (b - 1) + 1)
                            power(a_rs[:, 0:1], a_var[:, 0:1], 1).then_inc(a_rstd, 1)
                        if p == 3:
                            h_rows(b, 0)
                            pool.wait_ge(a_vare, TT * (b - 1) + 2)
                            power(a_rs[:, 1:2], a_var[:, 1:2], 1).then_inc(a_rstd, 1)
                        if p == 4:
                            h_rows(b, 1)
                            pool.wait_ge(h_vare, TT * (b - 1) + 1)
                            power(h_rs[:, 0:1], h_var[:, 0:1], 1).then_inc(h_rstd, 1)
                            pool.wait_ge(h_vare, TT * (b - 1) + 2)
                            power(h_rs[:, 1:2], h_var[:, 1:2], 1).then_inc(h_rstd, 1)
                        if p >= PAIRS - TT:
                            base_rows(b, p - PAIRS + TT)
                    for kind, j, bb in jobs_b(b, p - 1) + jobs_a(b, p):
                        if kind == "F1":
                            y_low(j, bb)
                    if isinstance(b, int):
                        for c in CHUNK_LOW.get((b, p), []):
                            split_chunk(c)

            batches(pool, batch)

        @block.scalar
        def _(act):
            a = nc.scalar

            def high(kind, j, b):
                bank = G_ps[bank_of(kind, j)]
                act.wait_ge(full[kind], count(kind, j, b))
                if kind == "X":
                    if not (isinstance(b, int) and b == -1):
                        act.wait_ge(full["Q"], 4 * (b + 1))
                    a.activation(xT_h[:, :, :].rearrange("p a n -> p (a n)"), bank[:, :],
                                 ACT.Copy).then_inc(xT_hi, 1)
                elif kind == "HT":
                    if not (isinstance(b, int) and b == 1):
                        act.wait_ge(full["F1"], 4 * (b - 1))
                    a.activation(hT_h[:, :, :].rearrange("p a n -> p (a n)"), bank[:, :],
                                 ACT.Copy).then_inc(hT_hi, 1)
                elif kind == "Q":
                    batch_before = b - lag(kind, j) - 1
                    if not (isinstance(b, int) and batch_before < 0):
                        act.wait_ge(scores_done, 2 * (PAIRS * batch_before + 2 * j + 2))
                    a.activation(q_sb[:, 2 * j:2 * j + 2, :].rearrange("p a n -> p (a n)"), bank[:, :],
                                 ACT.Copy, scale=-DH ** -0.5).then_inc(q_ready, 1)
                elif kind == "KV":
                    if not (isinstance(b, int) and b == -1):
                        act.wait_ge(scores_done, H * (b + 1))
                    a.activation(k_sb[:, 1:N + 1], bank[:, 0:N], ACT.Copy).then_inc(k_ready, 1)

            def hidden(j, b):
                n = count("F1", j, b) - 1
                act.wait_ge(u_ready, n + 1)
                if not (isinstance(n, int) and n < 2):
                    act.wait_ge(y_split, n - 1)
                elif j == 0:
                    chunk_split(act, 7)
                a.activation(t_buf[:, j % 2], u_buf[:, j % 2], ACT.Tanh, scale=0.5).then_inc(tanh_done, 1)

            def hidden_high(j, b):
                act.wait_ge(y_ready, count("F1", j, b))
                if j == 0 and not (isinstance(b, int) and b == 1):
                    act.wait_ge(full["F2"], TT * (b - 1))
                a.activation(y_h[:, 2 * j:2 * j + 2, :], t_buf[:, j % 2], ACT.Copy).then_inc(y_hi, 1)

            def exponentials(b, p):
                for i in range(2):
                    s = (2 * p + i) % RING
                    for qt, (c, w) in enumerate(((0, C0), (C0, C1))):
                        act.wait_ge(shifted, 4 * (PAIRS * b + p) + 2 * i + qt + 1)
                        a.activation(score[:, s, c:c + w], score[:, s, c:c + w], ACT.Exp,
                                     bias=neg_max[:, s, qt:qt + 1], scale=-1.0,
                                     accum_out=denom[:, s, qt:qt + 1]).then_inc(exp_done, 1)

            def normalise_even(b, p):
                s = (2 * p) % RING
                act.wait_ge(rdenom_done, PAIRS * b + p + 1)
                for qt, (c, w) in enumerate(((1, P), (C0 + 1, N))):
                    i = a.activation(score[:, s, c:c + w], score[:, s, c:c + w], ACT.Copy,
                                     scale=rdenom[:, s, qt:qt + 1])
                i.then_inc(even_done, 1)

            def even_transposed(b, p):
                n = PAIRS * b + p
                act.wait_ge(trans_done, n + 1)
                if not (isinstance(b, int) and n < 2):
                    act.wait_ge(pv_done, n - 1)
                a.activation(pT[:, 2 * (p % 2), :], T_ps[0][:, 0:N + P], ACT.Copy).then_inc(pT_even, 1)

            def o_high(b, p):
                n = PAIRS * b + p
                act.wait_ge(pv_done, n + 1)
                if p % PAIRS == 0 and not (isinstance(b, int) and n < PAIRS):
                    act.wait_ge(full["W"], TT * (b if p >= 0 else b - 1))
                a.activation(o_h[:, p % PAIRS, :], O_ps[:, 0:N], ACT.Identity,
                             bias=nv_col[:, :]).then_inc(o_hi, 1)

            def split_queries(c):
                act.wait_ge(stage_in[c], 16)
                cols = slice(c * INNER // 2, (c + 1) * INNER // 2)
                for kd in range(KD):
                    i = a.activation(wq_h[:, kd, cols], w_raw[c][:, kd * INNER // 2:(kd + 1) * INNER // 2],
                                     ACT.Identity, scale=gin_col[:, kd:kd + 1])
                i.then_inc(chunk_hi, 1)

            def split_chunk(c):
                dst, _ = chunk_dst(c)
                if c < 4:
                    act.wait_ge(stage_in[c % 2], 16 * (c // 2 + 1))
                else:
                    act.wait_ge(chunk_deq, c - 3)
                if c in (4, 5):
                    a.activation(dst, w_raw[c % 2], ACT.Identity, scale=gam_col[:, c - 4:c - 3]).then_inc(chunk_hi, 1)
                else:
                    a.activation(dst, w_raw[c % 2], ACT.Copy).then_inc(chunk_hi, 1)

            def batch(b):
                if isinstance(b, int) and b == -1:
                    act.dma_start(col_sb[:, :], columns).then_inc(cols_in, 16)
                    act.dma_start(mask_words[:, :], mask_rows[0:1, :].broadcast_to([P, N // 4])).then_inc(mask_in, 16)
                    act.wait_ge(halves_done, 1)
                    a.activation(denom[:, 0, :], halves[:, :], ACT.Exp)
                    for n, (lo, hi) in enumerate(BIAS_HEADS):
                        if n < 3:
                            act.dma_start(bias[:, lo:hi, :], bias_rows[:, lo:hi, :]).then_inc(bias_in[n], 16)
                        if n == 0:
                            act.dma_start(row_sb[:, :], rows.broadcast_to([P, 2 * DIM + DH])).then_inc(rows_in, 16)
                    act.wait_ge(cols_in, 16)
                    a.activation(k_sb[:, 0:1], nk_col, ACT.Copy).then_inc(nk_done, 1)
                    act.wait_ge(wkv_in, 32)
                    for kd in range(KD):
                        i = a.activation(wkv_h[:, kd, :], wkv_raw[:, kd, :], ACT.Identity,
                                         scale=gin_col[:, kd:kd + 1])
                    i.then_inc(wkv_hi, 1)
                    high("X", 0, b)
                    split_queries(0)
                    split_queries(1)
                    high("KV", 0, b)
                    high("Q", 0, b)
                    return
                for p in range(PAIRS):
                    late, early = jobs_b(b, p - 1), jobs_a(b, p)
                    if p != 3 and pair_runs(b, p - 3):
                        o_high(b, p - 3)
                    for kind, j, bb in late:
                        if kind in ("X", "Q", "KV", "HT"):
                            high(kind, j, bb)
                        if kind == "F1":
                            hidden(j, bb)
                    if attends(b):
                        exponentials(b, p)
                    if p == 3 and pair_runs(b, 0):
                        o_high(b, 0)
                    for kind, j, bb in late:
                        if kind == "F1":
                            hidden_high(j, bb)
                    for kind, j, bb in early:
                        if kind in ("X", "Q", "KV", "HT"):
                            high(kind, j, bb)
                        if kind == "F1":
                            hidden(j, bb)
                    if pair_runs(b, p - 1):
                        even_transposed(b, p - 1)
                    if attends(b):
                        normalise_even(b, p)
                    for kind, j, bb in early:
                        if kind == "F1":
                            hidden_high(j, bb)
                    if isinstance(b, int):
                        for c in CHUNK_HIGH.get((b, p), []):
                            split_chunk(c)

            batches(act, batch)

        @block.vector
        def _(dve):
            v = nc.vector

            def low(kind, j, b):
                bank = G_ps[bank_of(kind, j)]
                if kind == "X":
                    dve.wait_ge(xT_hi, b + 2)
                    v.tensor_tensor(xT_l[:, :, :].rearrange("p a n -> p (a n)"), bank[:, :],
                                    view(xT_h[:, :, :]).rearrange("p a n -> p (a n)"),
                                    ALU.subtract).then_inc(xT_split, 1)
                elif kind == "HT":
                    dve.wait_ge(hT_hi, b)
                    v.tensor_tensor(hT_l[:, :, :].rearrange("p a n -> p (a n)"), bank[:, :],
                                    view(hT_h[:, :, :]).rearrange("p a n -> p (a n)"),
                                    ALU.subtract).then_inc(hT_split, 1)
                elif kind == "KV":
                    dve.wait_ge(k_ready, b + 2)
                    if not (isinstance(b, int) and b == -1):
                        dve.wait_ge(v_ready, b + 1)
                    for t in range(TT):
                        i = v.tensor_tensor(v_next[:, t, :], bank[:, N + t * DH:N + (t + 1) * DH],
                                            nv_row[:, :], ALU.subtract)
                    i.then_inc(kv_ready, 1)
                elif kind == "W":
                    attention_stats(j, b)
                elif kind == "F1":
                    n = count("F1", j, b) - 1
                    if isinstance(n, int) and n < 2:
                        if j == 0:
                            dve.wait_ge(b1_done, 1)
                            chunk_split(dve, 7)
                    else:
                        dve.wait_ge(y_ready, n - 1)
                    dve.wait_ge(full["F1"], n + 1)
                    v.tensor_tensor(u_buf[:, j % 2], bank[:, :].rearrange("p (m n) -> p m n", m=2),
                                    b1_col[:, 2 * j:2 * j + 2].unsqueeze(2).broadcast_to([P, 2, N]),
                                    ALU.add).then_inc(u_ready, 1)
                elif kind == "F2":
                    n = TT * (b - 2) + j
                    dve.wait_ge(base_ready, n + 1)
                    if not (isinstance(b, int) and b == 2):
                        dve.wait_ge(out_sent, 16 * TT * (b - 2))
                    dve.wait_ge(full["F2"], n + 1)
                    v.scalar_tensor_tensor(out=out_sb[:, j, :], in0=bank[:, 0:DIM], scalar=0.25,
                                           in1=base[:, j, :], op0=ALU.mult, op1=ALU.add
                                           ).then_inc(out_ready, 1)

            def hidden_value(j, b):
                dve.wait_ge(tanh_done, count("F1", j, b))
                v.scalar_tensor_tensor(out=t_buf[:, j % 2], in0=t_buf[:, j % 2], scalar=1.0,
                                       in1=u_buf[:, j % 2], op0=ALU.add, op1=ALU.mult).then_inc(y_ready, 1)

            def aggregate(st, mv, var, t, stats, aggr, vare, n):
                dve.wait_ge(stats, n)
                gate(dve, dve_passed)
                v.bn_aggr(mv[:, t, :], st[:, t, :]).then_inc(aggr, 1)
                dve.wait_ge(aggr, n)
                v.tensor_scalar(var[:, t:t + 1], mv[:, t, 1:2], EPS, None, ALU.add).then_inc(vare, 1)

            def attention_stats(t, b):
                n = TT * (b - 1) + t + 1
                bank = G_ps[bank_of("W", t)]
                dve.wait_ge(full["W"], n)
                v.bn_stats(a_st[:, t, :], bank[:, 0:DIM]).then_inc(a_stats, 1)
                aggregate(a_st, a_mv, a_var, t, a_stats, a_aggr, a_vare, n)

            def attention_norm(t, b):
                n = TT * (b - 1) + t + 1
                bank = G_ps[bank_of("W", t)]
                dve.wait_ge(a_rstd, n)
                if t == 0:
                    if not (isinstance(b, int) and b == 1):
                        dve.wait_ge(base_ready, TT * (b - 1))
                    else:
                        chunk_split(dve, 7)
                v.tensor_scalar(hid[:, t, :], bank[:, 0:DIM], a_mv[:, t, 0:1], a_rs[:, t:t + 1],
                                ALU.subtract, ALU.mult).then_inc(a_normed, 1)

            def h_statistics(t, b):
                n = TT * (b - 1) + t + 1
                dve.wait_ge(h_ready, n)
                v.bn_stats(h_st[:, t, :], hid[:, t, :]).then_inc(h_stats, 1)
                aggregate(h_st, h_mv, h_var, t, h_stats, h_aggr, h_vare, n)

            def h_norm(t, b):
                n = TT * (b - 1) + t + 1
                dve.wait_ge(h_rstd, n)
                if t == 0 and not (isinstance(b, int) and b == 1):
                    dve.wait_ge(full["HT"], b - 1)
                v.tensor_scalar(hn[:, t, :], hid[:, t, :], h_mv[:, t, 0:1], h_rs[:, t:t + 1],
                                ALU.subtract, ALU.mult).then_inc(hn_ready, 1)

            def x_statistics(b):
                dve.wait_ge(x_in, 16 * (b + 2))
                for t in range(TT):
                    v.bn_stats(x_st[:, t, :], xs[:, t, :]).then_inc(x_stats, 1)
                dve.wait_ge(x_stats, TT * (b + 2))
                gate(dve, dve_passed)
                for t in range(TT):
                    v.bn_aggr(x_mv[:, t, :], x_st[:, t, :]).then_inc(x_aggr, 1)
                dve.wait_ge(x_aggr, TT * (b + 2))
                v.tensor_scalar(x_var[:, :], x_mv[:, :, 1], EPS, None, ALU.add).then_inc(x_vare, 1)

            def x_norm(b):
                dve.wait_ge(x_rstd, b + 2)
                if not (isinstance(b, int) and b == -1):
                    dve.wait_ge(full["X"], b + 1)
                for t in range(TT):
                    i = v.tensor_scalar(xn[:, t, :], xs[:, t, :], x_mv[:, t, 0:1], x_rs[:, t:t + 1],
                                        ALU.subtract, ALU.mult)
                i.then_inc(xn_ready, 1)

            def shift(b, p):
                n = PAIRS * b + p
                for i in range(2):
                    s = (2 * p + i) % RING
                    dve.wait_ge(scores_done, 2 * n + i + 1)
                    dve.wait_ge(score_bias, 2 * n + i + 1)
                    gate(dve, dve_passed)
                    for qt, (c, w) in enumerate(((0, C0), (C0, C1))):
                        v.tensor_tensor_reduce(
                            out=score[:, s, c:c + w], in0=S_ps[i][:, c:c + w], in1=score[:, s, c:c + w],
                            scale=1.0, scalar=3.0e38, op0=ALU.add, op1=ALU.min,
                            accum_out=neg_max[:, s, qt:qt + 1]).then_inc(shifted, 1)

            def denominators(b, p):
                s = (2 * p) % RING
                dve.wait_ge(exp_done, 4 * (PAIRS * b + p + 1))
                v.reciprocal(rdenom[:, s:s + 2, :], denom[:, s:s + 2, :]).then_inc(rdenom_done, 1)

            def normalise_odd(b, p):
                s = (2 * p + 1) % RING
                dve.wait_ge(rdenom_done, PAIRS * b + p + 1)
                for qt, (c, w) in enumerate(((1, P), (C0 + 1, N))):
                    i = v.tensor_scalar(score[:, s, c:c + w], score[:, s, c:c + w],
                                        rdenom[:, s, qt:qt + 1], None, ALU.mult)
                i.then_inc(odd_done, 1)

            def odd_transposed(b, p):
                n = PAIRS * b + p
                dve.wait_ge(trans_done, n + 1)
                if not (isinstance(b, int) and n < 2):
                    dve.wait_ge(pv_done, n - 1)
                v.tensor_copy(pT[:, 2 * (p % 2) + 1, :], T_ps[1][:, 0:N + P]).then_inc(pT_odd, 1)

            def o_low(b, p):
                n = PAIRS * b + p
                dve.wait_ge(o_hi, n + 1)
                v.scalar_tensor_tensor(out=o_l[:, p % PAIRS, :], in0=O_ps[:, 0:N], scalar=nv_col[:, :],
                                       in1=view(o_h[:, p % PAIRS, :]), op0=ALU.add,
                                       op1=ALU.subtract).then_inc(o_split, 1)

            def take_values(b):
                if not (isinstance(b, int) and b == 0):
                    dve.wait_ge(pv_done, PAIRS * b)
                dve.wait_ge(kv_ready, b + 1)
                v.tensor_copy(v_live[:, :, :], v_next[:, :, :]).then_inc(v_ready, 1)

            def dequantise(c):
                dve.wait_ge(stage_in[c % 2], 32 + 32 * ((c - 4) // 2 + 1))
                v.scalar_tensor_tensor(out=w_raw[c % 2], in0=w_raw[c % 2].bitcast(I32), scalar=-128.0,
                                       in1=s_raw[c % 2], op0=ALU.add, op1=ALU.mult).then_inc(chunk_deq, 1)

            def split_queries(c):
                cols = slice(c * INNER // 2, (c + 1) * INNER // 2)
                dve.wait_ge(chunk_hi, c + 1)
                for kd in range(KD):
                    i = v.scalar_tensor_tensor(
                        out=wq_l[:, kd, cols], in0=w_raw[c][:, kd * INNER // 2:(kd + 1) * INNER // 2],
                        scalar=gin_col[:, kd:kd + 1], in1=view(wq_h[:, kd, cols]), op0=ALU.mult,
                        op1=ALU.subtract)
                i.then_inc(half_done[c], 1)

            def split_w1(c):
                hi, lo = chunk_dst(c)
                dve.wait_ge(chunk_hi, c + 1)
                v.scalar_tensor_tensor(out=lo, in0=w_raw[c % 2], scalar=gam_col[:, c - 4:c - 3], in1=view(hi),
                                       op0=ALU.mult, op1=ALU.subtract).then_inc(half_done[c % 2], 1)

            def batch(b):
                if isinstance(b, int) and b == -1:
                    x_statistics(b)
                    x_norm(b)
                    dve.wait_ge(cols_in, 16)
                    dve.wait_ge(wkv_hi, 1)
                    for kd in range(KD):
                        i = v.scalar_tensor_tensor(out=wkv_l[:, kd, :], in0=wkv_raw[:, kd, :],
                                                   scalar=gin_col[:, kd:kd + 1], in1=view(wkv_h[:, kd, :]),
                                                   op0=ALU.mult, op1=ALU.subtract)
                    i.then_inc(wkv_done, 1)
                    low("X", 0, b)
                    split_queries(0)
                    dve.wait_ge(rows_in, 16)
                    v.tensor_scalar(b2_row, b2_row, 0.5, None, ALU.mult).then_inc(b2_half, 1)
                    low("KV", 0, b)
                    split_queries(1)
                    return
                for p in range(PAIRS):
                    late, early = jobs_b(b, p - 1), jobs_a(b, p)
                    if p != 3 and pair_runs(b, p - 3):
                        o_low(b, p - 3)
                    if p == 1 and inside(b, 0, B - 2):
                        x_norm(b)
                    if p == 2 and attends(b):
                        take_values(b)
                    if inside(b, 1, B):
                        if p == 3:
                            attention_norm(0, b)
                        if p == 4:
                            attention_norm(1, b)
                        if p == 5:
                            h_norm(0, b)
                            h_norm(1, b)
                    for job in late:
                        low(*job)
                    if attends(b):
                        shift(b, p)
                    for kind, j, bb in late:
                        if kind == "F1":
                            hidden_value(j, bb)
                    if p == 3 and pair_runs(b, 0):
                        o_low(b, 0)
                    for job in early:
                        low(*job)
                    if p == 0 and inside(b, 0, B - 2):
                        x_statistics(b)
                    if inside(b, 1, B):
                        if p == 3:
                            h_statistics(0, b)
                        if p == 4:
                            h_statistics(1, b)
                    if pair_runs(b, p - 1):
                        odd_transposed(b, p - 1)
                    if attends(b):
                        denominators(b, p)
                        normalise_odd(b, p)
                    for kind, j, bb in early:
                        if kind == "F1":
                            hidden_value(j, bb)
                    if isinstance(b, int):
                        for c in CHUNK_DEQUANTISE.get((b, p), []):
                            dequantise(c)
                        for c in W1_LOW.get((b, p), []):
                            split_w1(c)
                    if isinstance(b, int) and b == 0:
                        if p == SHIFT_STEP:
                            dve.wait_ge(full["BT"], 1)
                            v.tensor_tensor(b1_col[:, :], G_ps[bank_of(*SHIFT_SLOT)][:, ::SHIFT_COLS], b1_col[:, :],
                                            ALU.add).then_inc(b1_done, 1)

            batches(dve, batch)

        @block.tensor
        def _(pe):
            mm = nc.tensor.matmul

            def three(dst, lhs_h, lhs_l, rhs_h, rhs_l, first, last):
                mm(dst, lhs_h, rhs_h, start=first, stop=False)
                mm(dst, lhs_h, rhs_l, start=False, stop=False)
                return mm(dst, lhs_l, rhs_h, start=False, stop=last)

            def job(kind, j, b):
                bank = G_ps[bank_of(kind, j)]
                before = bank_before(kind, j, b)
                if before:
                    pe.wait_ge(emptied[before[0]], before[1])
                if kind == "X":
                    pe.wait_ge(xn_ready, b + 2)
                    for kd in range(KD):
                        for t in range(TT):
                            last = nc.tensor.transpose(bank[:, kd * N + t * P:kd * N + (t + 1) * P],
                                                       xn[:, t, kd * P:(kd + 1) * P], ident[:, :])
                elif kind == "HT":
                    pe.wait_ge(hn_ready, TT * b)
                    for kd in range(KD):
                        for t in range(TT):
                            last = nc.tensor.transpose(bank[:, kd * N + t * P:kd * N + (t + 1) * P],
                                                       hn[:, t, kd * P:(kd + 1) * P], ident[:, :])
                elif kind == "Q":
                    pe.wait_ge(xT_split, b - lag(kind, j) + 1)
                    for m in range(2):
                        cols = slice((2 * j + m) * P, (2 * j + m + 1) * P)
                        for kd in range(KD):
                            last = three(bank[:, m * N:(m + 1) * N], wq_h[:, kd, cols], wq_l[:, kd, cols],
                                         xT_h[:, kd, :], xT_l[:, kd, :], kd == 0, kd == KD - 1)
                elif kind == "KV":
                    pe.wait_ge(xT_split, b + 2)
                    for kd in range(KD):
                        three(bank[:, 0:N], wk_h[:, kd, :], wk_l[:, kd, :], xT_h[:, kd, :], xT_l[:, kd, :],
                              kd == 0, kd == KD - 1)
                    for t in range(TT):
                        rows = slice(t * P, (t + 1) * P)
                        for kd in range(KD):
                            last = three(bank[:, N + t * DH:N + (t + 1) * DH], xT_h[:, kd, rows],
                                         xT_l[:, kd, rows], wv_h[:, kd, :], wv_l[:, kd, :],
                                         kd == 0, kd == KD - 1)
                elif kind == "W":
                    rows = slice(j * P, (j + 1) * P)
                    if isinstance(b, int) and b == 1:
                        chunk_split(pe, 3)
                    for p in range(PAIRS):
                        if p == 0:
                            pe.wait_ge(o_split, PAIRS * b - 1)
                        if p == PAIRS - 1:
                            pe.wait_ge(o_split, PAIRS * b)
                        last = three(bank[:, 0:DIM], o_h[:, p, rows], o_l[:, p, rows], wo_h[:, p, :],
                                     wo_l[:, p, :], p == 0, p == PAIRS - 1)
                elif kind == "F1":
                    pe.wait_ge(hT_split, b - lag(kind, j) + 1)
                    if isinstance(b, int) and b == 1:
                        chunk_split(pe, 5)
                    for m in range(2):
                        cols = slice((2 * j + m) * P, (2 * j + m + 1) * P)
                        for kd in range(KD):
                            last = three(bank[:, m * N:(m + 1) * N], w1_h[:, kd, cols], w1_l[:, kd, cols],
                                         hT_h[:, kd, :], hT_l[:, kd, :], kd == 0, kd == KD - 1)
                elif kind == "F2":
                    rows = slice(j * P, (j + 1) * P)
                    for m in range(FM):
                        if m % 2 == 0:
                            pe.wait_ge(y_split, 4 * (b - 2) + m // 2 + 1)
                        last = three(bank[:, 0:DIM], y_h[:, m, rows], y_l[:, m, rows], w2_h[:, m, :],
                                     w2_l[:, m, :], m == 0, m == FM - 1)
                last.then_inc(full[kind], 1)

            def scores(b, p):
                n = PAIRS * b + p
                if not (isinstance(b, int) and n == 0):
                    pe.wait_ge(shifted, 4 * n)
                if p % 2 == 0:
                    pe.wait_ge(q_ready, 4 * b + p // 2 + 1)
                if p == 0:
                    pe.wait_ge(k_ready, b + 1)
                for qt, (a, w) in enumerate(((0, C0), (C0, C1))):
                    for i in range(2):
                        r = slice(DH * i, DH * (i + 1))
                        last = mm(S_ps[i][:, a:a + w], q_sb[r, p, qt * P:(qt + 1) * P], k_sb[r, 0:w],
                                  start=True, stop=True)
                        if qt == 1:
                            last.then_inc(scores_done, 1)

            def transposes(b, p):
                n = PAIRS * b + p
                if not (isinstance(b, int) and n == 0):
                    pe.wait_ge(pT_even, n)
                    pe.wait_ge(pT_odd, n)
                pe.wait_ge(even_done, n + 1)
                pe.wait_ge(odd_done, n + 1)
                for i in range(2):
                    s = (2 * p + i) % RING
                    for c, a in enumerate((1, C0 + 1, C0 + 1 + P)):
                        last = nc.tensor.transpose(T_ps[i][:, c * P:(c + 1) * P], score[:, s, a:a + P],
                                                   ident[:, :])
                last.then_inc(trans_done, 1)

            def values(b, p):
                n = PAIRS * b + p
                if not (isinstance(b, int) and n == 0):
                    pe.wait_ge(o_split, n)
                if p % PAIRS == 0:
                    pe.wait_ge(v_ready, b + 1)
                pe.wait_ge(pT_even, n + 1)
                pe.wait_ge(pT_odd, n + 1)
                gate(pe, pe_passed)
                for kt in range(2):
                    for i in range(2):
                        last = mm(O_ps[DH * i:DH * (i + 1), kt * P:N], v_live[:, kt, :],
                                  pT[:, 2 * (p % 2) + i, kt * N:N + kt * P], start=kt == 0, stop=kt == 1)
                last.then_inc(pv_done, 1)

            def warm_up(n):
                for _ in range(n):
                    nc.tensor.transpose(T_ps[1][:, 0:P], ident[:, :], ident[:, :])

            def shift_product():
                before = bank_before(*SHIFT_SLOT, 0)
                pe.wait_ge(emptied[before[0]], before[1])
                pe.wait_ge(chunk_deq, 2)
                for m in range(FM):
                    for kd in range(KD):
                        last = mm(G_ps[bank_of(*SHIFT_SLOT)][:, m * SHIFT_COLS:(m + 1) * SHIFT_COLS],
                                  w_raw[kd][:, m * P:(m + 1) * P],
                                  bet_col[:, kd:kd + 1].broadcast_to([P, SHIFT_COLS]),
                                  start=kd == 0, stop=kd == KD - 1)
                last.then_inc(full["BT"], 1)

            def batch(b):
                if isinstance(b, int) and b == -1:
                    pe.wait_ge(ident_done, 1)
                    warm_up(WARM_UP[0])
                    job("X", 0, b)
                    warm_up(WARM_UP[1])
                    pe.wait_ge(wkv_done, 1)
                    job("KV", 0, b)
                    pe.wait_ge(nk_done, 1)
                    chunk_split(pe, 0)
                    job("Q", 0, b)
                    return
                for p in range(PAIRS):
                    if attends(b):
                        scores(b, p)
                    if isinstance(b, int) and b == 0 and p == 1:
                        chunk_split(pe, 1)
                    for n in jobs_a(b, p):
                        job(*n)
                    if isinstance(b, int) and b == 0 and p == SHIFT_STEP:
                        shift_product()
                    if pair_runs(b, p - 1):
                        transposes(b, p - 1)
                    for n in jobs_b(b, p):
                        job(*n)
                    if pair_runs(b, p - 2):
                        values(b, p - 2)

            batches(pe, batch)


def kernel(**inputs):
    import numpy as np
    import concourse.bacc as bacc
    from concourse.bass_utils import run_bass_kernel_spmd

    def col(a):
        return np.reshape(a, (-1, P)).T

    v = {n.removeprefix("L0_"): np.asarray(a) for n, a in inputs.items()}
    null_k, null_v = v["cond_64"][0], v["cond_64"][1]
    bias, null = v["fside_16xSxS_0"], v["cond_null_attn_bias"]
    null = np.broadcast_to(null[None, :, None], (P, H, 1))
    arrays = {
        "x": v["x"],
        "bias_rows": np.concatenate([null, bias[:, :P, :P].transpose(1, 0, 2),
                                     null, bias[:, P:, :].transpose(1, 0, 2)], axis=2),
        "mask_rows": np.ascontiguousarray(v["mask_BxS_bk0"]).view(np.int32),
        "wq": v["cond_Wq"], "wkv": v["cond_Wkv"], "wo": v["cond_Wo"],
        "q1": v["ffn_fc1_q"], "s1": v["ffn_fc1_scales"],
        "q2": v["ffn_fc2_q"], "s2": v["ffn_fc2_scales"],
        "columns": np.concatenate([col(v["cond_g_in"]), col(v["ffn_ln_gamma"]), col(v["ffn_ln_beta"]),
                                   col(v["ffn_fc1_bias"]), col(np.tile(null_k, 2)),
                                   col(np.tile(null_v, 2))], axis=1),
        "rows": np.concatenate([v["cond_g_out"], v["ffn_fc2_bias"], null_v])[None, :],
    }
    nc = bacc.Bacc("TRN2", target_bir_lowering=False, num_devices=1)
    arrays = {n: np.ascontiguousarray(a) for n, a in arrays.items()}
    args = {n: nc.dram_tensor(f"in_{n}", a.shape, mybir.dt.from_np(a.dtype), kind="ExternalInput").ap()
            for n, a in arrays.items()}
    out = nc.dram_tensor("out_rows", (B, N, DIM), F32, kind="ExternalOutput").ap()
    build(nc, **args, out=out)
    r = run_bass_kernel_spmd(nc, [{f"in_{n}": a for n, a in arrays.items()}], core_ids=[0])
    return r.results[0]["out_rows"]
```

```python
from contextlib import ExitStack

import concourse.bass as bass
from concourse import mybir

ALU = mybir.AluOpType
ACT = mybir.ActivationFunctionType
F32 = mybir.dt.float32
F32R = mybir.dt.float32r
I32 = mybir.dt.int32
U8 = mybir.dt.uint8

P = 128
B, N, DIM = 8, 256, 256
H, DH = 16, 64
INNER = H * DH
F = 1024
EPS = 1e-5
BIG = 1.0e38
PAIRS = H // 2
KD = DIM // P
TT = N // P
FM = F // P
C0 = 1 + P
C1 = 1 + N
CS = C0 + C1
S1 = C0 + 1
RING = 8

STEADY = [
    (0, "A", "F1", 2, 2, 0), (0, "B", "Q", 3, 0, 1), (1, "A", "F1", 3, 2, 2), (1, "B", "X", 0, -1, 0),
    (2, "A", "W", 0, 1, 1), (3, "A", "Q", 0, -1, 2), (3, "A", "W", 1, 1, 0), (3, "B", "F2", 0, 2, 1),
    (4, "B", "Q", 1, -1, 2), (5, "A", "F2", 1, 2, 0), (5, "A", "HT", 0, 1, 1), (6, "A", "F1", 0, 1, 2),
    (6, "B", "Q", 2, -1, 0), (7, "A", "KV", 0, -1, 1), (7, "A", "F1", 1, 1, 2)]
SPECIAL = {
    -1: [(0, "A", "X", 0, -1, 0), (0, "A", "KV", 0, -1, 1), (0, "A", "Q", 0, -1, 2)],
    0: [(1, "A", "Q", 1, 0, 2), (2, "A", "Q", 2, 0, 0), (2, "A", "Q", 3, 0, 1), (2, "A", "X", 0, -1, 0),
        (3, "B", "Q", 0, -1, 2), (4, "A", "BT", 0, 0, 0), (4, "B", "Q", 1, -1, 2),
        (5, "B", "Q", 2, -1, 0), (6, "B", "KV", 0, -1, 1)],
    B - 1: [(0, "A", "F1", 2, 2, 0), (0, "B", "Q", 3, 0, 1), (1, "A", "F1", 3, 2, 2), (2, "A", "W", 0, 1, 1),
            (2, "B", "W", 1, 1, 0), (3, "A", "F2", 0, 2, 2), (3, "B", "F2", 1, 2, 1), (5, "A", "HT", 0, 1, 0),
            (6, "A", "F1", 0, 1, 2), (6, "A", "F1", 1, 1, 1), (7, "A", "F1", 2, 1, 0), (7, "B", "F1", 3, 1, 2)],
    B: [(2, "A", "W", 0, 1, 1), (3, "A", "W", 1, 1, 2), (3, "B", "F2", 0, 2, 0), (4, "B", "F2", 1, 2, 1),
        (5, "A", "HT", 0, 1, 0), (PAIRS, "A", "F1", 0, 1, 2), (PAIRS, "A", "F1", 1, 1, 1),
        (PAIRS, "A", "F1", 2, 1, 0), (PAIRS, "A", "F1", 3, 1, 2), (PAIRS, "A", "F2", 0, 1, 1),
        (PAIRS, "A", "F2", 1, 1, 0)],
    B + 1: []}
PER = {"F2": 2, "W": 2, "X": 1, "Q": 4, "HT": 1, "F1": 4, "KV": 1, "BT": 1}
G_BANKS = 3
Q_SCALE = -DH ** -0.5
WARM_UP = (20, 12)
STAY_WARM = (14, 14)
CHUNK_HIGH = {(0, 0): [2], (0, 1): [3], (0, 3): [4, 5], (0, 6): [6], (0, 7): [7]}
CHUNK_DEQUANTISE = {(0, 2): [4], (0, 3): [5], (0, 5): [6], (0, 6): [7]}
W1_LOW = {(0, 3): [4], (0, 4): [5]}
CHUNK_LOW = {(0, 0): [2], (0, 1): [3], (0, 7): [6], (1, 0): [7]}
SHIFT_COLS = 512 // FM


def timetable(b):
    if not isinstance(b, int):
        return [(p, side, kind, j, b - lag, bank) for p, side, kind, j, lag, bank in STEADY]
    return [(p, side, kind, j, b - lag, bank) for p, side, kind, j, lag, bank in SPECIAL.get(b, STEADY)
            if 0 <= b - lag < B]


def count(kind, j, c):
    return PER[kind] * c + j + 1


def bank_of(kind, j, b):
    return [bank for _, _, k, i, _, bank in timetable(b) if (k, i) == (kind, j)][0]


def bank_before(kind, j, c, b):
    jobs = timetable(b)
    here = [i for i, job in enumerate(jobs) if job[2] == kind and job[3] == j and same(job[4], c)][0]
    bank = jobs[here][5]
    earlier = [job for job in jobs[:here] if job[5] == bank]
    if not earlier and not (isinstance(b, int) and b < 0):
        earlier = [job for job in timetable(b - 1) if job[5] == bank]
    if not earlier:
        return None
    _, _, kind, j, c, _ = earlier[-1]
    return kind, count(kind, j, c)


def same(c, d):
    return not isinstance(c, int) or c == d


def build(nc, x, bias_rows, mask_rows, wq, wkv, wo, q1, s1, q2, s2, columns, rows, out):
    with ExitStack() as ctx:
        def sb(name, shape, dt=F32):
            return ctx.enter_context(nc.sbuf_tensor(name, shape, dt))

        def psum(name, shape, dt=F32):
            return ctx.enter_context(nc.psum_tensor(name, shape, dt))

        def sem(name):
            return ctx.enter_context(nc.semaphore(name))

        wq_h, wq_l = sb("wq_h", [P, KD, INNER], F32R), sb("wq_l", [P, KD, INNER], F32R)
        wkv_h, wkv_l = sb("wkv_h", [P, KD, 3 * DH], F32R), sb("wkv_l", [P, KD, 3 * DH], F32R)
        wk_h, wk_l, wv_h, wv_l = (wkv_h[:, :, 0:P], wkv_l[:, :, 0:P], wkv_h[:, :, P:], wkv_l[:, :, P:])
        wo_h, wo_l = sb("wo_h", [P, PAIRS, DIM], F32R), sb("wo_l", [P, PAIRS, DIM], F32R)
        w1_h, w1_l = sb("w1_h", [P, KD, F], F32R), sb("w1_l", [P, KD, F], F32R)
        w2_h, w2_l = sb("w2_h", [P, FM, DIM], F32R), sb("w2_l", [P, FM, DIM], F32R)
        xT_h, xT_l = sb("xT_h", [P, KD, N], F32R), sb("xT_l", [P, KD, N], F32R)
        hT_h, hT_l = sb("hT_h", [P, KD, N], F32R), sb("hT_l", [P, KD, N], F32R)
        q_sb, q_split = sb("q_sb", [P, PAIRS, P]), sb("q_split", [P, H, P], F32R)
        k_sb = sb("k_sb", [P, C0])
        k_h, k_l = sb("k_h", [P, C1 + 1], F32R), sb("k_l", [P, C1 + 1], F32R)
        o_h, o_l = sb("o_h", [P, PAIRS, N], F32R), sb("o_l", [P, PAIRS, N], F32R)
        y_h, y_l = sb("y_h", [P, FM, N], F32R), sb("y_l", [P, FM, N], F32R)
        bias = sb("bias", [P, H, CS])
        maskrow = sb("maskrow", [P, CS])
        mask_words = sb("mask_words", [P, N // 4], I32)
        score = sb("score", [P, RING, CS])
        neg_max = sb("neg_max", [P, RING, 2])
        denom = sb("denom", [P, RING, 2])
        rdenom = sb("rdenom", [P, RING, 2])
        pT = sb("pT", [P, 4, N + P])
        v_next = sb("v_next", [P, TT, DH])
        v_live = sb("v_live", [P, TT, DH])
        xs = sb("xs", [P, TT, DIM])
        xn = sb("xn", [P, TT, DIM])
        scratch = sb("scratch", [P, 16, DIM])
        u_buf = scratch[:, 0:4, :].rearrange("p (r m) n -> p r m n", r=2)
        t_buf = scratch[:, 4:8, :].rearrange("p (r m) n -> p r m n", r=2)
        bias_room = bias[:, :, :].rearrange("p h c -> p (h c)")
        u_last, t_last = (bias_room[:, i * FM * N:(i + 1) * FM * N].rearrange("p (r m n) -> p r m n", r=4, m=2)
                          for i in range(2))
        hid = scratch[:, 8:10, :]
        hn = scratch[:, 10:12, :]
        base = scratch[:, 12:14, :]
        xres = scratch[:, 14:16, :]
        w_raw = [scratch[:, 4 * i:4 * i + 4, :].rearrange("p a n -> p (a n)") for i in range(2)]
        s_raw = [scratch[:, 8 + 4 * i:12 + 4 * i, :].rearrange("p a n -> p (a n)") for i in range(2)]
        out_sb = sb("out_sb", [P, TT, DIM])
        row_sb = sb("row_sb", [P, 2 * DIM + DH])
        gout_row, b2_row, nv_row = (row_sb[:, 0:DIM], row_sb[:, DIM:2 * DIM],
                                    row_sb[:, 2 * DIM:2 * DIM + DH])
        wkv_raw = sb("wkv_raw", [P, KD, 3 * DH])
        col_sb = sb("col_sb", [P, 3 * KD + FM + 2])
        gin_col, gam_col, bet_col = (col_sb[:, KD * i:KD * (i + 1)] for i in range(3))
        b1_col = col_sb[:, 3 * KD:3 * KD + FM]
        nk_col, nv_col = (col_sb[:, 3 * KD + FM + i:3 * KD + FM + i + 1] for i in range(2))
        ident = sb("ident", [P, P])
        halves = sb("halves", [P, TT])
        x_st, x_mv, x_var, x_rs = (sb("x_st", [P, TT, 6]), sb("x_mv", [P, TT, 2]),
                                   sb("x_var", [P, TT]), sb("x_rs", [P, TT]))
        a_st, a_mv, a_var, a_rs = (sb("a_st", [P, TT, 6]), sb("a_mv", [P, TT, 2]),
                                   sb("a_var", [P, TT]), sb("a_rs", [P, TT]))
        h_st, h_mv, h_var, h_rs = (sb("h_st", [P, TT, 6]), sb("h_mv", [P, TT, 2]),
                                   sb("h_var", [P, TT]), sb("h_rs", [P, TT]))

        S_ps = [psum(f"S_ps{i}", [P, 512]) for i in range(2)]
        T_ps = [psum(f"T_ps{i}", [P, 512]) for i in range(2)]
        O_ps = psum("O_ps", [P, 512])
        G_ps = [psum(f"G_ps{i}", [P, 512]) for i in range(G_BANKS)]

        def view(t):
            return t.bitcast(F32)

        x_in, xres_in, mask_in = sem("x_in"), sem("xres_in"), sem("mask_in")
        cols_in, wkv_in, wq_in = sem("cols_in"), sem("wkv_in"), [sem("wq_in0"), sem("wq_in1")]
        rows_in = sem("rows_in")
        stage_in = [sem("stage_in0"), sem("stage_in1")]
        bias_in = [sem(f"bias_in{i}") for i in range(4)]
        out_sent = sem("out_sent")
        wkv_hi, wkv_done = sem("wkv_hi"), sem("wkv_done")
        chunk_deq, chunk_hi = sem("chunk_deq"), sem("chunk_hi")
        half_done = [sem("half_done0"), sem("half_done1")]
        ident_zero, ident_done, nk_done = sem("ident_zero"), sem("ident_done"), sem("nk_done")
        causal_done, halves_done, mask_edge = sem("causal_done"), sem("halves_done"), sem("mask_edge")
        b2_half, b1_done = sem("b2_half"), sem("b1_done")
        mask_ready, score_bias = sem("mask_ready"), sem("score_bias")
        scores_done, shifted, exp_done = sem("scores_done"), sem("shifted"), sem("exp_done")
        rdenom_done, even_done, odd_done, trans_done = (
            sem("rdenom_done"), sem("even_done"), sem("odd_done"), sem("trans_done"))
        pT_even, pT_odd, pv_done = sem("pT_even"), sem("pT_odd"), sem("pv_done")
        o_hi, o_split, v_ready = sem("o_hi"), sem("o_split"), sem("v_ready")
        full = {k: sem(f"{k}_full") for k in ("F2", "W", "X", "Q", "HT", "F1", "KV", "BT")}
        xT_hi, hT_hi, k_ready = sem("xT_hi"), sem("hT_hi"), sem("k_ready")
        q_hi, k_hi, nk_hi = sem("q_hi"), sem("k_hi"), sem("nk_hi")
        q_ready, kv_ready, xT_split, hT_split = (
            sem("q_ready"), sem("kv_ready"), sem("xT_split"), sem("hT_split"))
        a_normed, u_ready, out_ready = sem("a_normed"), sem("u_ready"), sem("out_ready")
        emptied = {"F2": out_ready, "W": a_normed, "X": xT_split, "Q": q_ready, "HT": hT_split,
                   "F1": u_ready, "KV": kv_ready, "BT": b1_done}
        x_stats, x_aggr, x_vare, x_rstd, xn_ready = (
            sem("x_stats"), sem("x_aggr"), sem("x_vare"), sem("x_rstd"), sem("xn_ready"))
        a_stats, a_aggr, a_vare, a_rstd = sem("a_stats"), sem("a_aggr"), sem("a_vare"), sem("a_rstd")
        h_ready, base_x, base_ready = sem("h_ready"), sem("base_x"), sem("base_ready")
        h_stats, h_aggr, h_vare, h_rstd, hn_ready = (
            sem("h_stats"), sem("h_aggr"), sem("h_vare"), sem("h_rstd"), sem("hn_ready"))
        tanh_done, y_ready, y_hi, y_split = (
            sem("tanh_done"), sem("y_ready"), sem("y_hi"), sem("y_split"))

        dve_passed, pool_passed, pe_passed = sem("dve_passed"), sem("pool_passed"), sem("pe_passed")

        block = ctx.enter_context(nc.Block())

        def batches(eng, batch):
            batch(-1)
            batch(0)
            batch(1)
            with eng.Fori(2, B - 1) as b:
                batch(b)
            batch(B - 1)
            batch(B)
            batch(B + 1)

        def inside(b, lo, hi):
            return not isinstance(b, int) or lo <= b <= hi

        def jobs_a(b, p):
            return [job[2:] for job in timetable(b) if job[0] == p and job[1] == "A"]

        def jobs_b(b, p):
            if p < 0:
                b, p = b - 1, p + PAIRS
                if isinstance(b, int) and b < 0:
                    return []
            return [job[2:] for job in timetable(b) if job[0] == p and job[1] == "B"]

        def last_bank(t):
            return [job[5] for job in timetable(B) if job[2:5] == ("F2", t, B - 1)][0]

        def is_last(c):
            return isinstance(c, int) and c == B - 1

        def u_slot(j, c):
            return u_last[:, j] if is_last(c) else u_buf[:, j % 2]

        def t_slot(j, c):
            return t_last[:, j] if is_last(c) else t_buf[:, j % 2]

        def attends(b):
            return inside(b, 0, B - 1)

        def steps(b):
            return range(2, PAIRS) if isinstance(b, int) and b == B else range(PAIRS)

        def pair_runs(b, p):
            return not isinstance(b, int) or 0 <= PAIRS * b + p < PAIRS * B

        def gate(eng, passed):
            eng.sem_inc(passed, 1)

        def chunk_src(c):
            if c < 2:
                r = wq.rearrange("(a p) n -> p a n", p=P)
                return r[:, :, c * INNER // 2:(c + 1) * INNER // 2]
            if c < 4:
                r = wo.rearrange("(a p) n -> p a n", p=P)
                return r[:, 4 * (c - 2):4 * (c - 1), :]
            if c < 6:
                return q1[(c - 4) * P:(c - 3) * P, :]
            r = q2.rearrange("(a p) n -> p a n", p=P)
            return r[:, 4 * (c - 6):4 * (c - 5), :]

        def chunk_scales(c):
            if c < 6:
                return s1[c - 4:c - 3, :].broadcast_to([P, F])
            r = s2[4 * (c - 6):4 * (c - 5), :]
            return r.rearrange("(o g) n -> o g n", o=1).broadcast_to([P, 4, DIM])

        def chunk_dst(c):
            if c < 4:
                s = slice(4 * (c - 2), 4 * (c - 1))
                return (wo_h[:, s, :].rearrange("p a n -> p (a n)"),
                        wo_l[:, s, :].rearrange("p a n -> p (a n)"))
            if c < 6:
                return w1_h[:, c - 4, :], w1_l[:, c - 4, :]
            s = slice(4 * (c - 6), 4 * (c - 5))
            return (w2_h[:, s, :].rearrange("p a n -> p (a n)"),
                    w2_l[:, s, :].rearrange("p a n -> p (a n)"))

        def chunk_split(eng, c):
            eng.wait_ge(half_done[c % 2], c // 2 + 1)
            if c > 0:
                eng.wait_ge(half_done[(c - 1) % 2], (c - 1) // 2 + 1)

        BIAS_HEADS = [(0, 2), (2, 4), (4, 8), (8, 16)]

        @block.sync
        def _(sp):
            def load_x(b):
                rows = x[b] if isinstance(b, int) else x[bass.ds(b, 1)].rearrange("o r c -> (o r) c")
                sp.dma_start(xs[:, :, :], rows.rearrange("(t p) c -> p t c", p=P)).then_inc(x_in, 16)

            def load_mask(b):
                src = mask_rows[b:b + 1, :] if isinstance(b, int) else mask_rows[bass.ds(b, 1), :]
                sp.dma_start(mask_words[:, :], src.broadcast_to([P, N // 4])).then_inc(mask_in, 16)

            def load_chunk(c):
                if c >= 2:
                    sp.wait_ge(half_done[c % 2], c // 2)
                dst = w_raw[c % 2] if c < 4 else w_raw[c % 2].bitcast(I32)
                if c < 2:
                    dst = dst.rearrange("p (a n) -> p a n", a=2)
                if 2 <= c < 4 or c >= 6:
                    dst = dst.rearrange("p (a n) -> p a n", a=4)
                if c >= 6:
                    sp.wait_ge(full["BT"], 1)
                sp.dma_start(dst, chunk_src(c)).then_inc(stage_in[c % 2], 16)
                if c >= 4:
                    d = s_raw[c % 2]
                    if c >= 6:
                        d = d.rearrange("p (a n) -> p a n", a=4)
                    sp.dma_start(d, chunk_scales(c)).then_inc(stage_in[c % 2], 16)

            def batch(b):
                if isinstance(b, int) and b == -1:
                    load_x(0)
                    wkv_rows = wkv.rearrange("(a p) n -> p a n", p=P)
                    sp.dma_start(wkv_raw[:, :, DH:], wkv_rows).then_inc(wkv_in, 16)
                    sp.dma_start(wkv_raw[:, :, 0:DH], wkv_rows[:, :, 0:DH]).then_inc(wkv_in, 16)
                    load_chunk(0)
                    load_chunk(1)
                    sp.wait_ge(xn_ready, 1)
                    load_x(1)
                    sp.wait_ge(mask_ready, 1)
                    load_mask(1)
                    load_chunk(2)
                    load_chunk(3)
                    lo, hi = BIAS_HEADS[3]
                    sp.dma_start(bias[:, lo:hi, :], bias_rows[:, lo:hi, :]).then_inc(bias_in[3], 16)
                    for c in range(4, 8):
                        load_chunk(c)
                    return
                if inside(b, 1, B - 2):
                    sp.wait_ge(xn_ready, b + 1)
                    load_x(b + 1)
                if inside(b, 1, B):
                    if not (isinstance(b, int) and b == 1):
                        sp.wait_ge(base_x, TT * (b - 1))
                    else:
                        chunk_split(sp, 7)
                    rows = x[b - 1] if isinstance(b, int) else \
                        x[bass.ds(b - 1, 1)].rearrange("o r c -> (o r) c")
                    sp.dma_start(xres, rows.rearrange("(t p) c -> p t c", p=P)).then_inc(xres_in, 16)
                if inside(b, 1, B - 2):
                    sp.wait_ge(mask_ready, b + 1)
                    load_mask(b + 1)
                if inside(b, 2, B + 1):
                    for t in range(TT):
                        sp.wait_ge(out_ready, TT * (b - 2) + t + 1)
                        rows = out[b - 2] if isinstance(b, int) else \
                            out[bass.ds(b - 2, 1)].rearrange("o r c -> (o r) c")
                        sp.dma_start(rows[t * P:(t + 1) * P, :], out_sb[:, t, :]).then_inc(out_sent, 16)

            batches(sp, batch)
            sp.wait_ge(out_sent, 16 * B * TT)

        @block.gpsimd
        def _(pool):
            g = nc.gpsimd

            def convert_mask(b):
                pool.wait_ge(mask_in, 16 * (b + 1))
                if not isinstance(b, int) or b > 0:
                    pool.wait_ge(score_bias, H * b)
                    gate(pool, pool_passed)
                for a, w in ((1, P), (C0 + 1, N)):
                    i = g.tensor_scalar(maskrow[:, a:a + w], mask_words[:, :].bitcast(U8)[:, 0:w], -BIG, BIG, ALU.mult, ALU.add)
                i.then_inc(mask_ready, 1)

            def bias_scores(b, p):
                for i in range(2):
                    h = 2 * p + i
                    if isinstance(b, int) and b == 0:
                        group = [n for n, (lo, hi) in enumerate(BIAS_HEADS) if lo <= h < hi][0]
                        pool.wait_ge(bias_in[group], 16)
                        fresh = i == 0
                        if fresh:
                            for a in (1, C0 + 1 + P):
                                blk = bias[:, h:h + 2, a:a + P]
                                c = g.affine_select(out=blk, in_=blk, pattern=[[0, 2], [-1, P]],
                                                    compare_op=ALU.is_ge, fill=-BIG, base=0,
                                                    channel_multiplier=1)
                                c.then_inc(causal_done, 1)
                        pool.wait_ge(causal_done, 2 * (p + 1))
                    if not (isinstance(b, int) and b == 0 and h < RING):
                        pool.wait_ge(trans_done, PAIRS * b + p - RING // 2 + 1)
                    if i == 0:
                        pool.wait_ge(mask_ready, b + 1)
                    g.tensor_tensor(score[:, h % RING, :], maskrow[:, :], bias[:, h, :],
                                    ALU.subtract).then_inc(score_bias, 1)

            def power(out_, in_, n):
                return g.tensor_tensor(out_, in_, halves[:, 0:n], ALU.pow)

            def h_rows(b, t):
                if isinstance(b, int) and b == B:
                    return
                """Gain of the attention's norm, then the residual's sum, of batch b-1."""
                pool.wait_ge(a_normed, TT * (b - 1) + t + 1)
                g.tensor_tensor(hid[:, t, :], hid[:, t, :], gout_row[:, :], ALU.mult).then_inc(h_ready, 1)

            def base_rows(b, t):
                if t == 0:
                    pool.wait_ge(xres_in, 16 * b)
                    if not (isinstance(b, int) and b < 2):
                        pool.wait_ge(out_ready, TT * (b - 1))
                    else:
                        pool.wait_ge(b2_half, 1)
                g.tensor_tensor(base[:, t, :], xres[:, t, :], b2_row[:, :], ALU.add).then_inc(base_x, 1)
                pool.wait_ge(base_x, TT * (b - 1) + t + 1)
                pool.wait_ge(h_ready, TT * (b - 1) + t + 1)
                g.tensor_tensor(base[:, t, :], base[:, t, :], hid[:, t, :], ALU.add).then_inc(base_ready, 1)

            def y_low(j, c):
                pool.wait_ge(y_hi, count("F1", j, c))
                g.tensor_tensor(y_l[:, 2 * j:2 * j + 2, :], t_slot(j, c), view(y_h[:, 2 * j:2 * j + 2, :]),
                                ALU.subtract).then_inc(y_split, 1)

            def split_chunk(c):
                hi, lo = chunk_dst(c)
                pool.wait_ge(chunk_hi, c + 1)
                g.tensor_tensor(lo, w_raw[c % 2], view(hi), ALU.subtract).then_inc(half_done[c % 2], 1)

            def x_power(b):
                pool.wait_ge(x_vare, b + 2)
                power(x_rs[:, :], x_var[:, :], TT).then_inc(x_rstd, 1)

            def batch(b):
                if isinstance(b, int) and b == -1:
                    g.memset(halves[:, :], -0.5).then_inc(halves_done, 1)
                    g.memset(maskrow[:, 0:CS:C0], 0.0).then_inc(mask_edge, 1)
                    g.memset(ident[:, :], 0.0).then_inc(ident_zero, 1)
                    pool.wait_ge(ident_zero, 1)
                    g.affine_select(out=ident[:, :], in_=ident[:, :], compare_op=ALU.not_equal, fill=1.0,
                                    base=0, pattern=[[-1, P]], channel_multiplier=1).then_inc(ident_done, 1)
                    pool.wait_ge(halves_done, 1)
                    x_power(b)
                    pool.wait_ge(mask_edge, 1)
                    convert_mask(0)
                    bias_scores(0, 0)
                    return
                for p in range(PAIRS):
                    if attends(b):
                        if p < PAIRS - 1:
                            bias_scores(b, p + 1)
                        elif inside(b, 0, B - 2):
                            convert_mask(b + 1)
                            bias_scores(b + 1, 0)
                    if inside(b, 0, B - 2) and p == 0:
                        x_power(b)
                    if inside(b, 1, B):
                        if p == 2:
                            pool.wait_ge(a_vare, TT * (b - 1) + 1)
                            power(a_rs[:, 0:1], a_var[:, 0:1], 1).then_inc(a_rstd, 1)
                        if p == 3:
                            h_rows(b, 0)
                            pool.wait_ge(a_vare, TT * (b - 1) + 2)
                            power(a_rs[:, 1:2], a_var[:, 1:2], 1).then_inc(a_rstd, 1)
                        if p == 4:
                            h_rows(b, 1)
                            pool.wait_ge(h_vare, TT * (b - 1) + 1)
                            power(h_rs[:, 0:1], h_var[:, 0:1], 1).then_inc(h_rstd, 1)
                            pool.wait_ge(h_vare, TT * (b - 1) + 2)
                            power(h_rs[:, 1:2], h_var[:, 1:2], 1).then_inc(h_rstd, 1)
                        if p >= PAIRS - TT:
                            base_rows(b, p - PAIRS + TT)
                    for kind, j, c, _ in jobs_b(b, p - 1) + jobs_a(b, p):
                        if kind == "F1":
                            y_low(j, c)
                    if isinstance(b, int):
                        for c in CHUNK_LOW.get((b, p), []):
                            split_chunk(c)
                if isinstance(b, int) and b == B:
                    for j in range(3):
                        y_low(j, B - 1)

            batches(pool, batch)

        @block.scalar
        def _(act):
            a = nc.scalar

            def high(kind, j, c, bank):
                act.wait_ge(full[kind], count(kind, j, c))
                first = isinstance(c, int) and c == 0
                if kind == "X":
                    if not first:
                        act.wait_ge(full["Q"], 4 * c)
                    a.activation(xT_h[:, :, :].rearrange("p a n -> p (a n)"), G_ps[bank][:, :],
                                 ACT.Copy).then_inc(xT_hi, 1)
                elif kind == "HT":
                    if not first:
                        act.wait_ge(full["F1"], 4 * c)
                    a.activation(hT_h[:, :, :].rearrange("p a n -> p (a n)"), G_ps[bank][:, :],
                                 ACT.Copy).then_inc(hT_hi, 1)
                elif kind == "Q":
                    if not first:
                        act.wait_ge(scores_done, 2 * (PAIRS * (c - 1) + 2 * j + 2))
                    rows = G_ps[bank][:, :].rearrange("p (a n) -> p a n", a=2)
                    a.activation(q_sb[:, 2 * j:2 * j + 2, :], rows[:, :, 0:P], ACT.Copy, scale=Q_SCALE)
                    for i in range(2):
                        r = slice(DH * i, DH * (i + 1))
                        last = a.activation(q_split[r, 4 * j + i:4 * j + 4:2, :], rows[r, :, P:N], ACT.Copy,
                                            scale=Q_SCALE)
                    last.then_inc(q_hi, 1)
                elif kind == "KV":
                    if not first:
                        act.wait_ge(scores_done, H * c)
                    a.activation(k_sb[:, 1:C0], G_ps[bank][:, 0:P], ACT.Copy)
                    a.activation(k_h[:, 1:C1], G_ps[bank][:, 0:N], ACT.Copy).then_inc(k_hi, 1)

            def hidden(j, c):
                n = count("F1", j, c) - 1
                act.wait_ge(u_ready, n + 1)
                if not is_last(c) and not (isinstance(n, int) and n < 2):
                    act.wait_ge(y_split, n - 1)
                elif j == 0 and not is_last(c):
                    chunk_split(act, 7)
                a.activation(t_slot(j, c), u_slot(j, c), ACT.Tanh, scale=0.5).then_inc(tanh_done, 1)

            def hidden_high(j, c):
                act.wait_ge(y_ready, count("F1", j, c))
                if j == 0 and not (isinstance(c, int) and c == 0):
                    act.wait_ge(full["F2"], TT * c)
                a.activation(y_h[:, 2 * j:2 * j + 2, :], t_slot(j, c), ACT.Copy).then_inc(y_hi, 1)

            def exponentials(b, p):
                for i in range(2):
                    s = (2 * p + i) % RING
                    for qt, (c, w) in enumerate(((0, C0), (C0, C1))):
                        act.wait_ge(shifted, 4 * (PAIRS * b + p) + 2 * i + qt + 1)
                        a.activation(score[:, s, c:c + w], score[:, s, c:c + w], ACT.Exp,
                                     bias=neg_max[:, s, qt:qt + 1], scale=-1.0,
                                     accum_out=denom[:, s, qt:qt + 1]).then_inc(exp_done, 1)

            def normalise_even(b, p):
                s = (2 * p) % RING
                act.wait_ge(rdenom_done, PAIRS * b + p + 1)
                for qt, (c, w) in enumerate(((1, P), (C0 + 1, N))):
                    i = a.activation(score[:, s, c:c + w], score[:, s, c:c + w], ACT.Copy,
                                     scale=rdenom[:, s, qt:qt + 1])
                i.then_inc(even_done, 1)

            def even_transposed(b, p):
                n = PAIRS * b + p
                act.wait_ge(trans_done, n + 1)
                if not (isinstance(b, int) and n < 2):
                    act.wait_ge(pv_done, n - 1)
                a.activation(pT[:, 2 * (p % 2), :], T_ps[0][:, 0:N + P], ACT.Copy).then_inc(pT_even, 1)

            def o_high(b, p):
                n = PAIRS * b + p
                act.wait_ge(pv_done, n + 1)
                if p % PAIRS == 0 and not (isinstance(b, int) and n < PAIRS):
                    act.wait_ge(full["W"], TT * (b if p >= 0 else b - 1))
                a.activation(o_h[:, p % PAIRS, :], O_ps[:, 0:N], ACT.Identity,
                             bias=nv_col[:, :]).then_inc(o_hi, 1)

            def split_queries(c):
                act.wait_ge(stage_in[c], 16)
                cols = slice(c * INNER // 2, (c + 1) * INNER // 2)
                for kd in range(KD):
                    i = a.activation(wq_h[:, kd, cols], w_raw[c][:, kd * INNER // 2:(kd + 1) * INNER // 2],
                                     ACT.Identity, scale=gin_col[:, kd:kd + 1])
                i.then_inc(chunk_hi, 1)

            def split_chunk(c):
                dst, _ = chunk_dst(c)
                if c < 4:
                    act.wait_ge(stage_in[c % 2], 16 * (c // 2 + 1))
                else:
                    act.wait_ge(chunk_deq, c - 3)
                if c in (4, 5):
                    a.activation(dst, w_raw[c % 2], ACT.Identity, scale=gam_col[:, c - 4:c - 3]).then_inc(chunk_hi, 1)
                else:
                    a.activation(dst, w_raw[c % 2], ACT.Copy).then_inc(chunk_hi, 1)

            def batch(b):
                if isinstance(b, int) and b == -1:
                    act.dma_start(col_sb[:, :], columns).then_inc(cols_in, 16)
                    act.dma_start(mask_words[:, :], mask_rows[0:1, :].broadcast_to([P, N // 4])).then_inc(mask_in, 16)
                    act.wait_ge(halves_done, 1)
                    a.activation(denom[:, 0, :], halves[:, :], ACT.Exp)
                    for n, (lo, hi) in enumerate(BIAS_HEADS):
                        if n < 3:
                            act.dma_start(bias[:, lo:hi, :], bias_rows[:, lo:hi, :]).then_inc(bias_in[n], 16)
                        if n == 0:
                            act.dma_start(row_sb[:, :], rows.broadcast_to([P, 2 * DIM + DH])).then_inc(rows_in, 16)
                    act.wait_ge(cols_in, 16)
                    a.activation(k_sb[:, 0:1], nk_col, ACT.Copy)
                    a.activation(k_h[:, 0:C1 + 1:C1], nk_col.broadcast_to([P, 2]), ACT.Copy).then_inc(nk_hi, 1)
                    act.wait_ge(wkv_in, 32)
                    for kd in range(KD):
                        i = a.activation(wkv_h[:, kd, :], wkv_raw[:, kd, :], ACT.Identity,
                                         scale=gin_col[:, kd:kd + 1])
                    i.then_inc(wkv_hi, 1)
                    high("X", 0, 0, bank_of("X", 0, b))
                    split_queries(0)
                    split_queries(1)
                    high("KV", 0, 0, bank_of("KV", 0, b))
                    high("Q", 0, 0, bank_of("Q", 0, b))
                    return
                if isinstance(b, int) and b == B:
                    last_pairs()
                for p in steps(b):
                    late, early = jobs_b(b, p - 1), jobs_a(b, p)
                    if p != 3 and pair_runs(b, p - 3) and inside(b, 0, B - 1):
                        o_high(b, p - 3)
                    for kind, j, c, bank in late:
                        if kind in ("X", "Q", "KV", "HT"):
                            high(kind, j, c, bank)
                        if kind == "F1":
                            hidden(j, c)
                    if attends(b):
                        exponentials(b, p)
                    for kind, j, c, _ in late:
                        if kind == "F1":
                            hidden_high(j, c)
                    for kind, j, c, bank in early:
                        if kind in ("X", "Q", "KV", "HT"):
                            high(kind, j, c, bank)
                        if kind == "F1":
                            hidden(j, c)
                    if p == 3 and pair_runs(b, 0):
                        o_high(b, 0)
                    if pair_runs(b, p - 1):
                        even_transposed(b, p - 1)
                    if attends(b):
                        normalise_even(b, p)
                    for kind, j, c, _ in early:
                        if kind == "F1":
                            hidden_high(j, c)
                    if isinstance(b, int):
                        for c in CHUNK_HIGH.get((b, p), []):
                            split_chunk(c)
                if isinstance(b, int) and b == B:
                    last_feed_forward()

            def last_pairs():
                o_high(B, -3)
                even_transposed(B, -1)
                o_high(B, -2)
                hidden(3, B - 2)
                o_high(B, -1)
                hidden_high(3, B - 2)

            def last_feed_forward():
                hidden(0, B - 1)
                for j in range(1, 4):
                    hidden(j, B - 1)
                    hidden_high(j - 1, B - 1)
                hidden_high(3, B - 1)

            batches(act, batch)

        @block.vector
        def _(dve):
            v = nc.vector

            def low(kind, j, c, g_bank):
                bank = G_ps[g_bank]
                first = isinstance(c, int) and c == 0
                if kind == "X":
                    dve.wait_ge(xT_hi, c + 1)
                    v.tensor_tensor(xT_l[:, :, :].rearrange("p a n -> p (a n)"), bank[:, :],
                                    view(xT_h[:, :, :]).rearrange("p a n -> p (a n)"),
                                    ALU.subtract).then_inc(xT_split, 1)
                elif kind == "HT":
                    dve.wait_ge(hT_hi, c + 1)
                    v.tensor_tensor(hT_l[:, :, :].rearrange("p a n -> p (a n)"), bank[:, :],
                                    view(hT_h[:, :, :]).rearrange("p a n -> p (a n)"),
                                    ALU.subtract).then_inc(hT_split, 1)
                elif kind == "KV":
                    dve.wait_ge(k_hi, c + 1)
                    v.tensor_tensor(k_l[:, 1:C1], bank[:, 0:N], view(k_h[:, 1:C1]), ALU.subtract
                                    ).then_inc(k_ready, 1)
                    if not first:
                        dve.wait_ge(v_ready, c)
                    for t in range(TT):
                        i = v.tensor_tensor(v_next[:, t, :], bank[:, N + t * DH:N + (t + 1) * DH],
                                            nv_row[:, :], ALU.subtract)
                    i.then_inc(kv_ready, 1)
                elif kind == "Q":
                    dve.wait_ge(q_hi, count("Q", j, c))
                    rows = bank[:, :].rearrange("p (a n) -> p a n", a=2)
                    for i in range(2):
                        own, other = slice(DH * i, DH * (i + 1)), slice(DH * (1 - i), DH * (2 - i))
                        heads = slice(4 * j + i, 4 * j + 4, 2)
                        last = v.scalar_tensor_tensor(
                            out=q_split[other, heads, :], in0=rows[own, :, P:N], scalar=Q_SCALE,
                            in1=view(q_split[own, heads, :]), op0=ALU.mult, op1=ALU.subtract)
                    last.then_inc(q_ready, 1)
                elif kind == "W":
                    attention_stats(j, c, bank)
                elif kind == "F1":
                    n = count("F1", j, c) - 1
                    if is_last(c):
                        if j == 0:
                            dve.wait_ge(score_bias, H * B)
                    elif isinstance(n, int) and n < 2:
                        if j == 0:
                            dve.wait_ge(b1_done, 1)
                            chunk_split(dve, 7)
                    else:
                        dve.wait_ge(y_ready, n - 1)
                    dve.wait_ge(full["F1"], n + 1)
                    v.tensor_tensor(u_slot(j, c), bank[:, :].rearrange("p (m n) -> p m n", m=2),
                                    b1_col[:, 2 * j:2 * j + 2].unsqueeze(2).broadcast_to([P, 2, N]),
                                    ALU.add).then_inc(u_ready, 1)
                elif kind == "F2":
                    n = TT * c + j
                    dve.wait_ge(base_ready, n + 1)
                    if not first:
                        dve.wait_ge(out_sent, 16 * TT * c)
                    dve.wait_ge(full["F2"], n + 1)
                    v.scalar_tensor_tensor(out=out_sb[:, j, :], in0=bank[:, 0:DIM], scalar=0.25,
                                           in1=base[:, j, :], op0=ALU.mult, op1=ALU.add
                                           ).then_inc(out_ready, 1)

            def shift_column():
                dve.wait_ge(full["BT"], 1)
                v.tensor_tensor(b1_col[:, :], G_ps[bank_of("BT", 0, 0)][:, ::SHIFT_COLS], b1_col[:, :],
                                ALU.add).then_inc(b1_done, 1)

            def hidden_value(j, c):
                dve.wait_ge(tanh_done, count("F1", j, c))
                v.scalar_tensor_tensor(out=t_slot(j, c), in0=t_slot(j, c), scalar=1.0,
                                       in1=u_slot(j, c), op0=ALU.add, op1=ALU.mult).then_inc(y_ready, 1)

            def aggregate(st, mv, var, t, stats, aggr, vare, n):
                dve.wait_ge(stats, n)
                gate(dve, dve_passed)
                v.bn_aggr(mv[:, t, :], st[:, t, :]).then_inc(aggr, 1)
                dve.wait_ge(aggr, n)
                v.tensor_scalar(var[:, t:t + 1], mv[:, t, 1:2], EPS, None, ALU.add).then_inc(vare, 1)

            def attention_stats(t, c, bank):
                n = TT * c + t + 1
                dve.wait_ge(full["W"], n)
                v.bn_stats(a_st[:, t, :], bank[:, 0:DIM]).then_inc(a_stats, 1)
                aggregate(a_st, a_mv, a_var, t, a_stats, a_aggr, a_vare, n)

            def attention_norm(t, b):
                n = TT * (b - 1) + t + 1
                bank = G_ps[bank_of("W", t, b)]
                dve.wait_ge(a_rstd, n)
                if t == 0:
                    if not (isinstance(b, int) and b == 1):
                        dve.wait_ge(base_ready, TT * (b - 1))
                    else:
                        chunk_split(dve, 7)
                v.tensor_scalar(hid[:, t, :], bank[:, 0:DIM], a_mv[:, t, 0:1], a_rs[:, t:t + 1],
                                ALU.subtract, ALU.mult).then_inc(a_normed, 1)
                if isinstance(b, int) and b == B:
                    dve.wait_ge(a_normed, n)
                    v.tensor_tensor(hid[:, t, :], hid[:, t, :], gout_row[:, :], ALU.mult).then_inc(h_ready, 1)

            def h_statistics(t, b):
                n = TT * (b - 1) + t + 1
                dve.wait_ge(h_ready, n)
                v.bn_stats(h_st[:, t, :], hid[:, t, :]).then_inc(h_stats, 1)
                aggregate(h_st, h_mv, h_var, t, h_stats, h_aggr, h_vare, n)

            def h_norm(t, b):
                n = TT * (b - 1) + t + 1
                dve.wait_ge(h_rstd, n)
                if t == 0 and not (isinstance(b, int) and b == 1):
                    dve.wait_ge(full["HT"], b - 1)
                v.tensor_scalar(hn[:, t, :], hid[:, t, :], h_mv[:, t, 0:1], h_rs[:, t:t + 1],
                                ALU.subtract, ALU.mult).then_inc(hn_ready, 1)

            def x_statistics(b):
                dve.wait_ge(x_in, 16 * (b + 2))
                for t in range(TT):
                    v.bn_stats(x_st[:, t, :], xs[:, t, :]).then_inc(x_stats, 1)
                dve.wait_ge(x_stats, TT * (b + 2))
                gate(dve, dve_passed)
                for t in range(TT):
                    v.bn_aggr(x_mv[:, t, :], x_st[:, t, :]).then_inc(x_aggr, 1)
                dve.wait_ge(x_aggr, TT * (b + 2))
                v.tensor_scalar(x_var[:, :], x_mv[:, :, 1], EPS, None, ALU.add).then_inc(x_vare, 1)

            def x_norm(b):
                dve.wait_ge(x_rstd, b + 2)
                if not (isinstance(b, int) and b == -1):
                    dve.wait_ge(full["X"], b + 1)
                for t in range(TT):
                    i = v.tensor_scalar(xn[:, t, :], xs[:, t, :], x_mv[:, t, 0:1], x_rs[:, t:t + 1],
                                        ALU.subtract, ALU.mult)
                i.then_inc(xn_ready, 1)

            def shift(b, p):
                n = PAIRS * b + p
                for i in range(2):
                    s = (2 * p + i) % RING
                    dve.wait_ge(scores_done, 2 * n + i + 1)
                    dve.wait_ge(score_bias, 2 * n + i + 1)
                    gate(dve, dve_passed)
                    for qt, (c, w, s0) in enumerate(((0, C0, 0), (C0, C1, S1))):
                        v.tensor_tensor_reduce(
                            out=score[:, s, c:c + w], in0=S_ps[i][:, s0:s0 + w], in1=score[:, s, c:c + w],
                            scale=1.0, scalar=3.0e38, op0=ALU.add, op1=ALU.min,
                            accum_out=neg_max[:, s, qt:qt + 1]).then_inc(shifted, 1)

            def denominators(b, p):
                s = (2 * p) % RING
                dve.wait_ge(exp_done, 4 * (PAIRS * b + p + 1))
                v.reciprocal(rdenom[:, s:s + 2, :], denom[:, s:s + 2, :]).then_inc(rdenom_done, 1)

            def normalise_odd(b, p):
                s = (2 * p + 1) % RING
                dve.wait_ge(rdenom_done, PAIRS * b + p + 1)
                for qt, (c, w) in enumerate(((1, P), (C0 + 1, N))):
                    i = v.tensor_scalar(score[:, s, c:c + w], score[:, s, c:c + w],
                                        rdenom[:, s, qt:qt + 1], None, ALU.mult)
                i.then_inc(odd_done, 1)

            def odd_transposed(b, p):
                n = PAIRS * b + p
                dve.wait_ge(trans_done, n + 1)
                if not (isinstance(b, int) and n < 2):
                    dve.wait_ge(pv_done, n - 1)
                v.tensor_copy(pT[:, 2 * (p % 2) + 1, :], T_ps[1][:, 0:N + P]).then_inc(pT_odd, 1)

            def o_low(b, p):
                n = PAIRS * b + p
                dve.wait_ge(o_hi, n + 1)
                v.scalar_tensor_tensor(out=o_l[:, p % PAIRS, :], in0=O_ps[:, 0:N], scalar=nv_col[:, :],
                                       in1=view(o_h[:, p % PAIRS, :]), op0=ALU.add,
                                       op1=ALU.subtract).then_inc(o_split, 1)

            def take_values(b):
                if not (isinstance(b, int) and b == 0):
                    dve.wait_ge(pv_done, PAIRS * b)
                dve.wait_ge(kv_ready, b + 1)
                v.tensor_copy(v_live[:, :, :], v_next[:, :, :]).then_inc(v_ready, 1)

            def dequantise(c):
                dve.wait_ge(stage_in[c % 2], 32 + 32 * ((c - 4) // 2 + 1))
                v.scalar_tensor_tensor(out=w_raw[c % 2], in0=w_raw[c % 2].bitcast(I32), scalar=-128.0,
                                       in1=s_raw[c % 2], op0=ALU.add, op1=ALU.mult).then_inc(chunk_deq, 1)

            def split_queries(c):
                cols = slice(c * INNER // 2, (c + 1) * INNER // 2)
                dve.wait_ge(chunk_hi, c + 1)
                for kd in range(KD):
                    i = v.scalar_tensor_tensor(
                        out=wq_l[:, kd, cols], in0=w_raw[c][:, kd * INNER // 2:(kd + 1) * INNER // 2],
                        scalar=gin_col[:, kd:kd + 1], in1=view(wq_h[:, kd, cols]), op0=ALU.mult,
                        op1=ALU.subtract)
                i.then_inc(half_done[c], 1)

            def split_w1(c):
                hi, lo = chunk_dst(c)
                dve.wait_ge(chunk_hi, c + 1)
                v.scalar_tensor_tensor(out=lo, in0=w_raw[c % 2], scalar=gam_col[:, c - 4:c - 3], in1=view(hi),
                                       op0=ALU.mult, op1=ALU.subtract).then_inc(half_done[c % 2], 1)

            def batch(b):
                if isinstance(b, int) and b == -1:
                    x_statistics(b)
                    x_norm(b)
                    dve.wait_ge(cols_in, 16)
                    dve.wait_ge(wkv_hi, 1)
                    for kd in range(KD):
                        i = v.scalar_tensor_tensor(out=wkv_l[:, kd, :], in0=wkv_raw[:, kd, :],
                                                   scalar=gin_col[:, kd:kd + 1], in1=view(wkv_h[:, kd, :]),
                                                   op0=ALU.mult, op1=ALU.subtract)
                    i.then_inc(wkv_done, 1)
                    low("X", 0, 0, bank_of("X", 0, b))
                    split_queries(0)
                    dve.wait_ge(rows_in, 16)
                    v.tensor_scalar(b2_row, b2_row, 0.5, None, ALU.mult).then_inc(b2_half, 1)
                    dve.wait_ge(nk_hi, 1)
                    v.tensor_tensor(k_l[:, 0:C1 + 1:C1], nk_col.broadcast_to([P, 2]), view(k_h[:, 0:C1 + 1:C1]),
                                    ALU.subtract).then_inc(nk_done, 1)
                    low("KV", 0, 0, bank_of("KV", 0, b))
                    split_queries(1)
                    low("Q", 0, 0, bank_of("Q", 0, b))
                    return
                if isinstance(b, int) and b == B:
                    last_pairs()
                for p in steps(b):
                    late, early = jobs_b(b, p - 1), jobs_a(b, p)
                    if p == 1 and inside(b, 0, B - 2):
                        x_norm(b)
                    if p == 2 and attends(b):
                        take_values(b)
                    if inside(b, 1, B):
                        if p == 3:
                            attention_norm(0, b)
                        if p == 4:
                            attention_norm(1, b)
                        if p == 5:
                            h_norm(0, b)
                            h_norm(1, b)
                    if attends(b):
                        shift(b, p)
                    if p != 3 and pair_runs(b, p - 3) and inside(b, 0, B - 1):
                        o_low(b, p - 3)
                    for job in late + early:
                        low(*job)
                    if p == 3 and pair_runs(b, 0):
                        o_low(b, 0)
                    for kind, j, c, _ in late:
                        if kind == "F1":
                            hidden_value(j, c)
                    if p == 0 and inside(b, 0, B - 2):
                        x_statistics(b)
                    if inside(b, 1, B):
                        if p == 3:
                            h_statistics(0, b)
                        if p == 4:
                            h_statistics(1, b)
                    if pair_runs(b, p - 1):
                        odd_transposed(b, p - 1)
                    if attends(b):
                        denominators(b, p)
                        normalise_odd(b, p)
                    for kind, j, c, _ in early:
                        if kind == "F1":
                            hidden_value(j, c)
                    if isinstance(b, int):
                        for c in CHUNK_DEQUANTISE.get((b, p), []):
                            dequantise(c)
                        for c in W1_LOW.get((b, p), []):
                            split_w1(c)
                    if ("BT", 0, b, bank_of("BT", 0, 0)) in early:
                        shift_column()
                if isinstance(b, int) and b == B:
                    last_feed_forward()

            def last_pairs():
                o_low(B, -3)
                odd_transposed(B, -1)
                low("F1", 3, B - 2, bank_of("F1", 3, B - 1))
                o_low(B, -2)
                hidden_value(3, B - 2)
                o_low(B, -1)

            def last_feed_forward():
                def part(j):
                    low("F1", j, B - 1, bank_of("F1", j, B))

                part(0)
                for j in range(1, 4):
                    part(j)
                    hidden_value(j - 1, B - 1)
                hidden_value(3, B - 1)
                dve.wait_ge(y_split, count("F1", 2, B - 1))
                dve.wait_ge(y_hi, count("F1", 3, B - 1))
                v.tensor_tensor(y_l[:, 6:8, :], t_last[:, 3], view(y_h[:, 6:8, :]),
                                ALU.subtract).then_inc(y_split, 1)
                for t in range(TT):
                    low("F2", t, B - 1, last_bank(t))

            batches(dve, batch)

        @block.tensor
        def _(pe):
            mm = nc.tensor.matmul

            def three(dst, lhs_h, lhs_l, rhs_h, rhs_l, first, last):
                mm(dst, lhs_h, rhs_h, start=first, stop=False)
                mm(dst, lhs_h, rhs_l, start=False, stop=False)
                return mm(dst, lhs_l, rhs_h, start=False, stop=last)

            def job(kind, j, c, g_bank, b, tiles=None):
                bank = G_ps[g_bank]
                before = bank_before(kind, j, c, b)
                if before and not (tiles and 0 not in tiles):
                    pe.wait_ge(emptied[before[0]], before[1])
                if kind == "X":
                    pe.wait_ge(xn_ready, c + 1)
                    for kd in range(KD):
                        for t in range(TT):
                            last = nc.tensor.transpose(bank[:, kd * N + t * P:kd * N + (t + 1) * P],
                                                       xn[:, t, kd * P:(kd + 1) * P], ident[:, :])
                elif kind == "HT":
                    pe.wait_ge(hn_ready, TT * (c + 1))
                    for kd in range(KD):
                        for t in range(TT):
                            last = nc.tensor.transpose(bank[:, kd * N + t * P:kd * N + (t + 1) * P],
                                                       hn[:, t, kd * P:(kd + 1) * P], ident[:, :])
                elif kind == "Q":
                    pe.wait_ge(xT_split, c + 1)
                    for m in range(2):
                        cols = slice((2 * j + m) * P, (2 * j + m + 1) * P)
                        for kd in range(KD):
                            last = three(bank[:, m * N:(m + 1) * N], wq_h[:, kd, cols], wq_l[:, kd, cols],
                                         xT_h[:, kd, :], xT_l[:, kd, :], kd == 0, kd == KD - 1)
                elif kind == "KV":
                    pe.wait_ge(xT_split, c + 1)
                    for kd in range(KD):
                        three(bank[:, 0:N], wk_h[:, kd, :], wk_l[:, kd, :], xT_h[:, kd, :], xT_l[:, kd, :],
                              kd == 0, kd == KD - 1)
                    for t in range(TT):
                        rows = slice(t * P, (t + 1) * P)
                        for kd in range(KD):
                            last = three(bank[:, N + t * DH:N + (t + 1) * DH], xT_h[:, kd, rows],
                                         xT_l[:, kd, rows], wv_h[:, kd, :], wv_l[:, kd, :],
                                         kd == 0, kd == KD - 1)
                elif kind == "W":
                    rows = slice(j * P, (j + 1) * P)
                    if isinstance(c, int) and c == 0:
                        chunk_split(pe, 3)
                    for p in range(PAIRS):
                        if p == 0:
                            pe.wait_ge(o_split, PAIRS * (c + 1) - 1)
                        if p == PAIRS - 1:
                            pe.wait_ge(o_split, PAIRS * (c + 1))
                        last = three(bank[:, 0:DIM], o_h[:, p, rows], o_l[:, p, rows], wo_h[:, p, :],
                                     wo_l[:, p, :], p == 0, p == PAIRS - 1)
                elif kind == "BT":
                    pe.wait_ge(chunk_deq, 2)
                    for m in range(FM):
                        for kd in range(KD):
                            last = mm(bank[:, m * SHIFT_COLS:(m + 1) * SHIFT_COLS],
                                      w_raw[kd][:, m * P:(m + 1) * P],
                                      bet_col[:, kd:kd + 1].broadcast_to([P, SHIFT_COLS]),
                                      start=kd == 0, stop=kd == KD - 1)
                elif kind == "F1":
                    pe.wait_ge(hT_split, c + 1)
                    if isinstance(c, int) and c == 0:
                        chunk_split(pe, 5)
                    for m in range(2):
                        cols = slice((2 * j + m) * P, (2 * j + m + 1) * P)
                        for kd in range(KD):
                            last = three(bank[:, m * N:(m + 1) * N], w1_h[:, kd, cols], w1_l[:, kd, cols],
                                         hT_h[:, kd, :], hT_l[:, kd, :], kd == 0, kd == KD - 1)
                elif kind == "F2":
                    rows = slice(j * P, (j + 1) * P)
                    for m in tiles or range(FM):
                        if m % 2 == 0:
                            pe.wait_ge(y_split, 4 * c + m // 2 + 1)
                        last = three(bank[:, 0:DIM], y_h[:, m, rows], y_l[:, m, rows], w2_h[:, m, :],
                                     w2_l[:, m, :], m == 0, m == FM - 1)
                if not tiles or FM - 1 in tiles:
                    last.then_inc(full[kind], 1)

            def scores(b, p):
                n = PAIRS * b + p
                if not (isinstance(b, int) and n == 0):
                    pe.wait_ge(shifted, 4 * n)
                if p % 2 == 0:
                    pe.wait_ge(q_ready, 4 * b + p // 2 + 1)
                if p == 0:
                    pe.wait_ge(k_ready, b + 1)
                for i in range(2):
                    r = slice(DH * i, DH * (i + 1))
                    mm(S_ps[i][:, 0:C0], q_sb[r, p, :], k_sb[r, :], start=True, stop=True)
                for i in range(2):
                    q = q_split[:, 2 * p + i, :]
                    tile_1 = S_ps[i][:, S1:S1 + C1 + 1]
                    mm(tile_1, q, k_h[:, :], start=True, stop=False)
                    mm(tile_1, q, k_l[:, :], start=False, stop=True).then_inc(scores_done, 1)

            def transposes(b, p):
                n = PAIRS * b + p
                if not (isinstance(b, int) and n == 0):
                    pe.wait_ge(pT_even, n)
                    pe.wait_ge(pT_odd, n)
                pe.wait_ge(even_done, n + 1)
                pe.wait_ge(odd_done, n + 1)
                for i in range(2):
                    s = (2 * p + i) % RING
                    for c, a in enumerate((1, C0 + 1, C0 + 1 + P)):
                        last = nc.tensor.transpose(T_ps[i][:, c * P:(c + 1) * P], score[:, s, a:a + P],
                                                   ident[:, :])
                last.then_inc(trans_done, 1)

            def values(b, p):
                n = PAIRS * b + p
                if not (isinstance(b, int) and n == 0):
                    pe.wait_ge(o_split, n)
                if p % PAIRS == 0:
                    pe.wait_ge(v_ready, b + 1)
                pe.wait_ge(pT_even, n + 1)
                pe.wait_ge(pT_odd, n + 1)
                gate(pe, pe_passed)
                for kt in range(2):
                    for i in range(2):
                        last = mm(O_ps[DH * i:DH * (i + 1), kt * P:N], v_live[:, kt, :],
                                  pT[:, 2 * (p % 2) + i, kt * N:N + kt * P], start=kt == 0, stop=kt == 1)
                last.then_inc(pv_done, 1)

            def warm_up(n):
                for _ in range(n):
                    nc.tensor.transpose(T_ps[1][:, 0:P], ident[:, :], ident[:, :])

            def batch(b):
                if isinstance(b, int) and b == -1:
                    pe.wait_ge(ident_done, 1)
                    warm_up(WARM_UP[0])
                    job("X", 0, 0, bank_of("X", 0, b), b)
                    warm_up(WARM_UP[1])
                    pe.wait_ge(wkv_done, 1)
                    job("KV", 0, 0, bank_of("KV", 0, b), b)
                    pe.wait_ge(nk_done, 1)
                    chunk_split(pe, 0)
                    job("Q", 0, 0, bank_of("Q", 0, b), b)
                    return
                for p in range(PAIRS):
                    if attends(b):
                        scores(b, p)
                    if isinstance(b, int) and b == 0 and p == 1:
                        chunk_split(pe, 1)
                    if isinstance(b, int) and b == B and p == 0:
                        job("F2", 0, B - 2, bank_of("F2", 0, B), B, range(FM - 4))
                    if isinstance(b, int) and b == B and p == 5:
                        warm_up(STAY_WARM[0])
                    for n in jobs_a(b, p):
                        job(*n, b, rest(n, b))
                    if pair_runs(b, p - 1):
                        transposes(b, p - 1)
                    for n in jobs_b(b, p):
                        job(*n, b, rest(n, b))
                    if pair_runs(b, p - 2):
                        values(b, p - 2)
                    if isinstance(b, int) and b == B and p == 0:
                        job("F2", 0, B - 2, bank_of("F2", 0, B), B, range(FM - 4, FM - 2))
                if isinstance(b, int) and b == B:
                    warm_up(STAY_WARM[1])
                    last_feed_forward()

            def rest(job_, b):
                return range(FM - 2, FM) if isinstance(b, int) and b == B and job_[:2] == ("F2", 0) else None

            def last_feed_forward():
                for j in range(4):
                    job("F1", j, B - 1, bank_of("F1", j, B), B)
                for tiles in (range(m, m + 2) for m in range(0, FM, 2)):
                    for t in range(TT):
                        job("F2", t, B - 1, last_bank(t), B, tiles)

            batches(pe, batch)


def kernel(**inputs):
    import numpy as np
    import concourse.bacc as bacc
    from concourse.bass_utils import run_bass_kernel_spmd

    def col(a):
        return np.reshape(a, (-1, P)).T

    v = {n.removeprefix("L0_"): np.asarray(a) for n, a in inputs.items()}
    null_k, null_v = v["cond_64"][0], v["cond_64"][1]
    bias, null = v["fside_16xSxS_0"], v["cond_null_attn_bias"]
    null = np.broadcast_to(null[None, :, None], (P, H, 1))
    arrays = {
        "x": v["x"],
        "bias_rows": np.concatenate([null, bias[:, :P, :P].transpose(1, 0, 2),
                                     null, bias[:, P:, :].transpose(1, 0, 2)], axis=2),
        "mask_rows": np.ascontiguousarray(v["mask_BxS_bk0"]).view(np.int32),
        "wq": v["cond_Wq"], "wkv": v["cond_Wkv"], "wo": v["cond_Wo"],
        "q1": v["ffn_fc1_q"], "s1": v["ffn_fc1_scales"],
        "q2": v["ffn_fc2_q"], "s2": v["ffn_fc2_scales"],
        "columns": np.concatenate([col(v["cond_g_in"]), col(v["ffn_ln_gamma"]), col(v["ffn_ln_beta"]),
                                   col(v["ffn_fc1_bias"]), col(np.tile(null_k, 2)),
                                   col(np.tile(null_v, 2))], axis=1),
        "rows": np.concatenate([v["cond_g_out"], v["ffn_fc2_bias"], null_v])[None, :],
    }
    nc = bacc.Bacc("TRN2", target_bir_lowering=False, num_devices=1)
    arrays = {n: np.ascontiguousarray(a) for n, a in arrays.items()}
    args = {n: nc.dram_tensor(f"in_{n}", a.shape, mybir.dt.from_np(a.dtype), kind="ExternalInput").ap()
            for n, a in arrays.items()}
    out = nc.dram_tensor("out_rows", (B, N, DIM), F32, kind="ExternalOutput").ap()
    build(nc, **args, out=out)
    r = run_bass_kernel_spmd(nc, [{f"in_{n}": a for n, a in arrays.items()}], core_ids=[0])
    return r.results[0]["out_rows"]
```
